# Optimizing a Trainium2 kernel written in Bass

```python
import numpy as np
import jax
import jax.numpy as jnp

def _softmax(x, axis=-1):
    return jax.nn.softmax(x, axis=axis)

def _gelu(x):
    return jax.nn.gelu(x, approximate=True)

def _silu(x):
    return jax.nn.silu(x)

def _sigmoid(x):
    return jax.nn.sigmoid(x)

def _layernorm(x, axis=-1, eps=1e-05):
    m = jnp.mean(x, axis=axis, keepdims=True)
    v = jnp.var(x, axis=axis, keepdims=True)
    return (x - m) / jnp.sqrt(v + eps)

def _scatter_add(tgt, idx, src, axis=0):
    return tgt.at[idx].add(src)

def _segment_sum(src, seg, n):
    return jax.ops.segment_sum(src, seg, n)
kernel_name = 'mk_recurrent_d1_jaxref_r4_b42087'

def setup_inputs(seed: int=0):
    np.random.seed(seed)
    _w = jnp.asarray

    def _L0_attn_setup():
        import jax, jax.numpy as jnp
        import numpy as np
        EMBED = 1024
        HEADS = 16
        HEAD_DIM = EMBED // HEADS
        ROT = 64
        B, S = (1, 512)
        MASK_VAL = -1000000000.0

        def _rotate_every_two(x):
            r = jnp.stack((x[..., 1::2], x[..., ::2]), axis=-1)
            return r.reshape(x.shape)

        def _fixed_pos_embedding(seq_len, rot_dim):
            inv_freq = 1.0 / 10000.0 ** (jnp.arange(0, rot_dim, 2, dtype=jnp.float32) / rot_dim)
            t = jnp.arange(seq_len, dtype=jnp.float32)
            sinusoid = jnp.einsum('i,j->ij', t, inv_freq)
            return (jnp.sin(sinusoid), jnp.cos(sinusoid))

        def _apply_rotary(x, sin, cos):
            sin = jnp.repeat(sin[None, :, None, :], 2, axis=3)
            cos = jnp.repeat(cos[None, :, None, :], 2, axis=3)
            return x * cos + _rotate_every_two(x) * sin
        key = jax.random.key(seed)
        ks = jax.random.split(key, 5)
        sc = 0.02
        return {'hidden_states': jax.random.normal(ks[0], (B, S, EMBED), jnp.float32), 'Wq': jax.random.normal(ks[1], (EMBED, EMBED), jnp.float32) * sc, 'Wk': jax.random.normal(ks[2], (EMBED, EMBED), jnp.float32) * sc, 'Wv': jax.random.normal(ks[3], (EMBED, EMBED), jnp.float32) * sc, 'Wo': jax.random.normal(ks[4], (EMBED, EMBED), jnp.float32) * sc}
    _L0_attn_in = _L0_attn_setup()

    def _L0_ffn_setup():
        import jax, jax.numpy as jnp
        import numpy as np

        @jax.custom_vjp
        def ste_sign(w):
            return jnp.sign(w)

        def _ste_fwd(w):
            return (jnp.sign(w), w)

        def _ste_bwd(w, g):
            mask = ((w > -1) & (w < 1)).astype(g.dtype)
            return (g * mask,)
        ste_sign.defvjp(_ste_fwd, _ste_bwd)
        key = jax.random.key(seed)
        k = jax.random.split(key, 6)
        B, S, H, O, E = (4, 512, 1024, 1024, 8)
        return {'x': jax.random.normal(k[0], (B, S, H), dtype=jnp.float32), 'weight': jax.random.normal(k[1], (O, H), dtype=jnp.float32) * 0.02, 'bias': jax.random.normal(k[2], (O,), dtype=jnp.float32) * 0.02, 'gate_w': jax.random.normal(k[3], (E, H), dtype=jnp.float32) * 0.02, 'in_channel_scale': jax.random.normal(k[4], (E, H), dtype=jnp.float32), 'out_channel_scale': jax.random.normal(k[5], (E, O), dtype=jnp.float32)}
    _L0_ffn_in = _L0_ffn_setup()
    _d = {'L0_attn_hidden_states': _L0_attn_in['hidden_states'], 'L0_attn_Wq': _L0_attn_in['Wq'], 'L0_attn_Wk': _L0_attn_in['Wk'], 'L0_attn_Wv': _L0_attn_in['Wv'], 'L0_attn_Wo': _L0_attn_in['Wo'], 'L0_ffn_weight': _L0_ffn_in['weight'], 'L0_ffn_bias': _L0_ffn_in['bias'], 'L0_ffn_gate_w': _L0_ffn_in['gate_w'], 'L0_ffn_in_channel_scale': _L0_ffn_in['in_channel_scale'], 'L0_ffn_out_channel_scale': _L0_ffn_in['out_channel_scale']}
    _x0 = _d['L0_attn_hidden_states']
    _d['L0_attn_hidden_states'] = jax.random.normal(jax.random.fold_in(jax.random.key(seed), 1), (4, 512, 1024), dtype=_x0.dtype)
    del _x0
    return _d

def reference(L0_attn_hidden_states, L0_attn_Wq, L0_attn_Wk, L0_attn_Wv, L0_attn_Wo, L0_ffn_weight, L0_ffn_bias, L0_ffn_gate_w, L0_ffn_in_channel_scale, L0_ffn_out_channel_scale):

    def _L0_attn_ref(hidden_states, Wq, Wk, Wv, Wo):
        import jax, jax.numpy as jnp
        import numpy as np
        EMBED = 1024
        HEADS = 16
        HEAD_DIM = EMBED // HEADS
        ROT = 64
        B, S = (1, 512)
        MASK_VAL = -1000000000.0

        def _rotate_every_two(x):
            r = jnp.stack((x[..., 1::2], x[..., ::2]), axis=-1)
            return r.reshape(x.shape)

        def _fixed_pos_embedding(seq_len, rot_dim):
            inv_freq = 1.0 / 10000.0 ** (jnp.arange(0, rot_dim, 2, dtype=jnp.float32) / rot_dim)
            t = jnp.arange(seq_len, dtype=jnp.float32)
            sinusoid = jnp.einsum('i,j->ij', t, inv_freq)
            return (jnp.sin(sinusoid), jnp.cos(sinusoid))

        def _apply_rotary(x, sin, cos):
            sin = jnp.repeat(sin[None, :, None, :], 2, axis=3)
            cos = jnp.repeat(cos[None, :, None, :], 2, axis=3)
            return x * cos + _rotate_every_two(x) * sin
        b, s, e = hidden_states.shape
        q = (hidden_states @ Wq).reshape(b, s, HEADS, HEAD_DIM)
        k = (hidden_states @ Wk).reshape(b, s, HEADS, HEAD_DIM)
        v = (hidden_states @ Wv).reshape(b, s, HEADS, HEAD_DIM)
        sin, cos = _fixed_pos_embedding(s, ROT)
        q = jnp.concatenate([_apply_rotary(q[..., :ROT], sin, cos), q[..., ROT:]], axis=-1)
        k = jnp.concatenate([_apply_rotary(k[..., :ROT], sin, cos), k[..., ROT:]], axis=-1)
        q = q.transpose(0, 2, 1, 3)
        k = k.transpose(0, 2, 1, 3)
        v = v.transpose(0, 2, 1, 3)
        logits = jnp.einsum('bhqd,bhkd->bhqk', q, k)
        causal = jnp.tril(jnp.ones((s, s), dtype=bool))[None, None]
        logits = jnp.where(causal, logits, MASK_VAL)
        logits = logits / jnp.sqrt(jnp.float32(HEAD_DIM))
        attn = jax.nn.softmax(logits, axis=-1)
        out = jnp.einsum('bhqk,bhkd->bhqd', attn, v)
        out = out.transpose(0, 2, 1, 3).reshape(b, s, e)
        return out @ Wo

    def _L0_ffn_ref(x, weight, bias, gate_w, in_channel_scale, out_channel_scale):
        import jax, jax.numpy as jnp
        import numpy as np

        @jax.custom_vjp
        def ste_sign(w):
            return jnp.sign(w)

        def _ste_fwd(w):
            return (jnp.sign(w), w)

        def _ste_bwd(w, g):
            mask = ((w > -1) & (w < 1)).astype(g.dtype)
            return (g * mask,)
        ste_sign.defvjp(_ste_fwd, _ste_bwd)
        B, S, H = x.shape
        xf = x.reshape(-1, H)
        router_logits = xf @ gate_w.T
        routing = jax.nn.softmax(router_logits.astype(jnp.float32), axis=1).astype(x.dtype)
        in_scale = routing @ in_channel_scale
        out_scale = routing @ out_channel_scale
        wb = ste_sign(weight)
        out = xf * in_scale @ wb.T * out_scale + bias
        return out.reshape(B, S, -1)
    x = L0_attn_hidden_states
    xn = _layernorm(x, axis=-1)
    s = _L0_attn_ref(xn, L0_attn_Wq, L0_attn_Wk, L0_attn_Wv, L0_attn_Wo)
    g = _silu(_L0_ffn_ref(xn, L0_ffn_weight, L0_ffn_bias, L0_ffn_gate_w, L0_ffn_in_channel_scale, L0_ffn_out_channel_scale))
    x = x + s * g
    return x

_drawn_inputs = setup_inputs


def setup_inputs(seed=0):
    import zlib

    import numpy as np

    out = dict(_drawn_inputs(seed))
    spreads = {}
    factors = {'L0_ffn_bias': 64.0}
    for name, (base, spread) in spreads.items():
        noise = np.random.default_rng([zlib.crc32(name.encode()), seed]).standard_normal(out[name].shape)
        drawn = base * np.exp(spread * noise) if base else spread * noise
        out[name] = jnp.asarray(drawn.astype(out[name].dtype))
    for name, factor in factors.items():
        out[name] = (out[name] * factor).astype(out[name].dtype)
    return out
```

```python
from contextlib import ExitStack

import concourse.bass as bass
from concourse import mybir

F32 = mybir.dt.float32
F32R = mybir.dt.float32r
BF16 = mybir.dt.bfloat16
ALU = mybir.AluOpType
ACT = mybir.ActivationFunctionType
AX = mybir.AxisListType

P = 128
BATCH, SEQ, EMBED = 4, 512, 1024
KT = EMBED // P
QT = SEQ // P
HEADS, HEAD_DIM = 16, 64
PAIRS = HEADS // 2
EXPERTS = 8
HALF = EMBED // 2
LN_EPS = 1e-5
STEPS = 2 * 2 * PAIRS
MASK = -1.0e9 / 8.0
PHI, PLO = 0, 1

SCORE_BANKS = (((3, 0),), ((2, 0), (0, 384)), ((1, 0),))
PT_BANKS = (((0, 0),), ((1, 0), (3, 384)), ((2, 0),))
PT_WIDTH = (512, 512, 256)
P_COL = {3: 0, 2: 512, 0: 896, 1: 1024}
PT_COL = {0: 0, 1: 512, 3: 896, 2: 1024}


def raw(ap):
    return ap.bitcast(F32)


def split_matmuls(pe, out, hi_lo_stationary, hi_lo_moving, first=True, final=True):
    (sh, sl), (mh, ml) = hi_lo_stationary, hi_lo_moving
    pe.matmul(out, sh, mh, start=first, stop=False)
    pe.matmul(out, sh, ml, start=False, stop=False)
    return pe.matmul(out, sl, mh, start=False, stop=final)


def setup_block(nc, io, keep):
    with ExitStack() as ctx:
        def sb(name, shape, dt):
            return ctx.enter_context(nc.sbuf_tensor(name, shape, dt))

        def sem(name):
            return ctx.enter_context(nc.semaphore(name))

        w_rows = sb("su_w_rows", [P, 4, EMBED], F32)
        w_sign = sb("su_w_sign", [P, 2, EMBED], BF16)
        gate_rows = sb("su_gate_rows", [EXPERTS, EMBED], F32)
        chan_rows = sb("su_chan_rows", [P, 2, EMBED], F32)
        tr_ps = [ctx.enter_context(nc.psum_tensor(f"su_tr{i}", [P, KT, P], BF16)) for i in range(2)]
        gate_ps = ctx.enter_context(nc.psum_tensor("su_gate_ps", [P, KT, EXPERTS], F32))

        w_in = [sem(f"su_w_in{i}") for i in range(4)]
        small_in, gate_in = sem("su_small_in"), sem("su_gate_in")
        zeroed, idents, ident_copies = sem("su_zeroed"), sem("su_idents"), sem("su_ident_copies")
        signed, sign_tr, sign_copied = sem("su_signed"), sem("su_sign_tr"), sem("su_sign_copied")
        gate_tr, gate_hi, chan_hi, finished = sem("su_gate_tr"), sem("su_gate_hi"), sem("su_chan_hi"), sem("su_finished")
        block = ctx.enter_context(nc.Block())

        @block.sync
        def _(sp):
            for t in range(KT):
                if t >= 4:
                    sp.wait_ge(signed, t - 3)
                sp.dma_start(w_rows[:, t % 4, :], io["weight"][t * P:(t + 1) * P, :]).then_inc(w_in[t % 4], 16)
            sp.dma_start(gate_rows[:], io["gate_w"]).then_inc(gate_in, 16)
            sp.dma_start(keep["bias"][:], io["bias"].rearrange("(a n) -> a n", a=1).to_broadcast([P, EMBED])).then_inc(small_in, 16)
            sp.wait_ge(zeroed, 1)
            for c, table in enumerate((io["in_scale"], io["out_scale"])):
                for r in range(4):
                    sp.dma_start(chan_rows[32 * r:32 * r + EXPERTS, c, :], table).then_inc(small_in, 16)
            sp.wait_ge(small_in, 9 * 16)

        @block.gpsimd
        def _(pool):
            pool.memset(chan_rows[:], 0.0).then_inc(zeroed, 1)
            pool.memset(keep["ident"][:], 0.0).then_inc(idents, 1)
            pool.wait_ge(idents, 1)
            pool.affine_select(out=keep["ident"][:], in_=keep["ident"][:], compare_op=ALU.not_equal, fill=1.0,
                               base=0, pattern=[[-1, P]], channel_multiplier=1).then_inc(idents, 1)
            pool.memset(keep["causal"][:], 0.0).then_inc(idents, 1)
            pool.wait_ge(idents, 3)
            pool.affine_select(out=keep["causal"][:], in_=keep["causal"][:], compare_op=ALU.is_ge, fill=MASK,
                               base=0, pattern=[[-1, P]], channel_multiplier=1).then_inc(idents, 1)

        @block.scalar
        def _(act):
            for t in range(KT):
                act.wait_ge(w_in[t % 4], 16 * (t // 4 + 1))
                if t >= 2:
                    act.wait_ge(sign_tr, t - 1)
                act.activation(w_sign[:, t % 2, :], w_rows[:, t % 4, :], ACT.Sign).then_inc(signed, 1)
            act.wait_ge(gate_tr, 1)
            act.activation(keep["gate_t"][:, :, 0:EXPERTS], gate_ps[:], ACT.Copy).then_inc(gate_hi, 1)
            act.wait_ge(small_in, 9 * 16)
            for c, name in enumerate(("chan_in", "chan_out")):
                act.activation(keep[name][:], chan_rows[:, c, :], ACT.Copy).then_inc(chan_hi, 1)

        @block.tensor
        def _(pe):
            pe.wait_ge(ident_copies, 2)
            for t in range(KT):
                pe.wait_ge(signed, t + 1)
                if t >= 2:
                    pe.wait_ge(sign_copied, t - 1)
                for k in range(KT):
                    last = pe.transpose(tr_ps[t % 2][:, k, :], w_sign[:, t % 2, k * P:(k + 1) * P], keep["ident_bf"][:])
                last.then_inc(sign_tr, 1)
            pe.wait_ge(gate_in, 16)
            pe.wait_ge(idents, 2)
            for k in range(KT):
                last = pe.transpose(gate_ps[:, k, :], gate_rows[:, k * P:(k + 1) * P], keep["ident"][0:EXPERTS, 0:EXPERTS])
            last.then_inc(gate_tr, 1)

        @block.vector
        def _(dve):
            dve.wait_ge(idents, 2)
            dve.tensor_copy(keep["ident_r"][:], keep["ident"][:]).then_inc(ident_copies, 1)
            dve.tensor_copy(keep["ident_bf"][:], keep["ident"][:]).then_inc(ident_copies, 1)
            for t in range(KT):
                dve.wait_ge(sign_tr, t + 1)
                dve.tensor_copy(keep["sign_t"][:, :, t * P:(t + 1) * P], tr_ps[t % 2][:]).then_inc(sign_copied, 1)
            dve.wait_ge(gate_hi, 1)
            dve.tensor_tensor(keep["gate_t"][:, :, EXPERTS:2 * EXPERTS], gate_ps[:],
                              raw(keep["gate_t"][:, :, 0:EXPERTS]), ALU.subtract).then_inc(finished, 1)
            dve.wait_ge(chan_hi, 2)
            for c, name in enumerate(("chan_in", "chan_out")):
                for r in (1, 3):
                    rows = slice(32 * r, 32 * r + 32)
                    dve.tensor_tensor(keep[name][rows, :], chan_rows[rows, c, :], raw(keep[name][rows, :]),
                                      ALU.subtract).then_inc(finished, 1)


def ffn_block(nc, io, keep, xn, xn_store, z_store):
    with ExitStack() as ctx:
        def sb(name, shape, dt):
            return ctx.enter_context(nc.sbuf_tensor(name, shape, dt))

        def psum(name, shape):
            return ctx.enter_context(nc.psum_tensor(name, shape, F32))

        def sem(name):
            return ctx.enter_context(nc.semaphore(name))

        x_tile = sb("ff_x", [P, 2, EMBED], F32)
        stats = sb("ff_stats", [P, 2, 2, 6], F32)
        moments = sb("ff_moments", [P, 2, 2], F32)
        ln = sb("ff_ln", [P, 2, 8], F32)
        logit_t = sb("ff_logit_t", [2 * EXPERTS, SEQ], F32)
        parts = sb("ff_parts", [P, QT, 2 * EXPERTS], F32)
        route = sb("ff_route", [P, QT, EXPERTS], F32)
        route_e = sb("ff_route_e", [P, QT, EXPERTS], F32)
        route_m = sb("ff_route_m", [P, 3, QT], F32)
        route4 = sb("ff_route4", [P, QT, P], F32R)
        route_t = sb("ff_route_t", [P, 2, SEQ], F32R)
        xn_sum = sb("ff_xn_sum", [P, 2, SEQ], F32)
        xs_full = sb("ff_xs_full", [P, 2, SEQ], F32)
        xs_hi = sb("ff_xs_hi", [P, KT, SEQ], F32R)
        xs_lo = sb("ff_xs_lo", [P, KT, SEQ], F32R)
        out_sc = sb("ff_out_sc", [P, 2, HALF], F32)
        z = sb("ff_z", [P, 2, EMBED], F32)

        tr_ps = psum("ff_tr", [P, 2, 4, P])
        small_ps = psum("ff_small", [P, SEQ])
        z_ps = [psum(f"ff_z_ps{i}", [P, 2, HALF]) for i in range(2)]
        osc_ps = psum("ff_osc_ps", [P, HALF])

        x_in = [sem(f"ff_x_in{i}") for i in range(2)]
        ln_a, ln_var, ln_sqrt, normed = sem("ff_ln_a"), sem("ff_ln_var"), sem("ff_ln_sqrt"), sem("ff_normed")
        x_tr, x_hi, x_lo, xn_out = sem("ff_x_tr"), sem("ff_x_hi"), sem("ff_x_lo"), [sem(f"ff_xn_out{i}") for i in range(2)]
        gate_mm, gate_sb, gate_tr = sem("ff_gate_mm"), sem("ff_gate_sb"), sem("ff_gate_tr")
        rt, shifted, expd, route_ok, route_tr, route_sb = (sem("ff_rt"), sem("ff_shifted"), sem("ff_expd"), sem("ff_route_ok"),
                                                        sem("ff_route_tr"), sem("ff_route_sb"))
        zeroed = sem("ff_zeroed")
        sc_mm, summed, scaled, xs_h, xs_l = sem("ff_sc_mm"), sem("ff_summed"), sem("ff_scaled"), sem("ff_xs_h"), sem("ff_xs_l")
        z_mm, osc_mm, osc_sb, z_mul, z_add = sem("ff_z_mm"), sem("ff_osc_mm"), sem("ff_osc_sb"), sem("ff_z_mul"), sem("ff_z_add")
        z_out = [sem(f"ff_z_out{i}") for i in range(2)]
        block = ctx.enter_context(nc.Block())

        @block.sync
        def _(sp):
            def load(n):
                if n >= 2:
                    sp.wait_ge(x_tr, 2 * (n - 1))
                sp.dma_start(x_tile[:, n % 2, :], io["x"][n * P:(n + 1) * P, :]).then_inc(x_in[n % 2], 16)

            def store_xn(j):
                sp.wait_ge(x_lo, 8 * (j + 1))
                sp.dma_start(xn_store[j, :, 0, :, :], raw(xn[j][PHI][:])).then_inc(xn_out[j], 16)
                sp.dma_start(xn_store[j, :, 1, :, :], raw(xn[j][PLO][:])).then_inc(xn_out[j], 16)

            def store_z(n):
                sp.wait_ge(z_add, n + 1)
                sp.dma_start(z_store[n * P:(n + 1) * P, :], z[:, n % 2, :]).then_inc(z_out[n % 2], 16)

            for n in range(QT):
                load(n)
            for j in range(BATCH):
                if j < 2:
                    store_xn(j)
                if j + 1 < BATCH:
                    for t in range(QT):
                        load(QT * (j + 1) + t)
                        if t == 1:
                            store_z(QT * j)
                    for t in range(1, QT):
                        store_z(QT * j + t)
                else:
                    for t in range(QT):
                        store_z(QT * j + t)
            for i in range(2):
                sp.wait_ge(z_out[i], 16 * 8)
                sp.wait_ge(xn_out[i], 32)

        @block.tensor
        def _(pe):
            def x_transposes(n):
                pe.wait_ge(normed, n + 1)
                for b in range(2):
                    if n >= 1:
                        pe.wait_ge(x_lo, 2 * (n - 1) + b + 1)
                    if n >= QT and n % QT == 0:
                        pe.wait_ge(scaled, KT * (n // QT))
                    for k in range(4):
                        last = pe.transpose(tr_ps[:, b, k, :], x_tile[:, n % 2, (4 * b + k) * P:(4 * b + k + 1) * P],
                                            keep["ident"][:])
                    last.then_inc(x_tr, 1)

            def gate(j):
                hi, lo = xn[j % 2]
                pe.wait_ge(x_lo, 8 * (j + 1))
                if j >= 1:
                    pe.wait_ge(route_sb, j)
                for k in range(KT):
                    pe.matmul(small_ps[0:2 * EXPERTS, :], keep["gate_t"][:, k, :], hi[:, k, :], start=(k == 0), stop=False)
                    last = pe.matmul(small_ps[0:2 * EXPERTS, :], keep["gate_t"][:, k, :], lo[:, k, :], start=False, stop=(k == KT - 1))
                last.then_inc(gate_mm, 1)
                pe.wait_ge(gate_sb, 2 * j + 1)
                for t in range(QT):
                    last = pe.transpose(small_ps[:, 16 * t:16 * t + 16], logit_t[:, t * P:(t + 1) * P],
                                        keep["ident"][0:2 * EXPERTS, 0:2 * EXPERTS])
                last.then_inc(gate_tr, 1)

            def route_transposes(j):
                pe.wait_ge(route_ok, 2 * (j + 1))
                for t in range(QT):
                    last = pe.transpose(small_ps[:, t * P:(t + 1) * P].bitcast(F32R), route4[:, t, :], keep["ident_r"][:])
                last.then_inc(route_tr, 1)

            def in_scale(j):
                pe.wait_ge(route_sb, j + 1)
                pe.wait_ge(x_lo, 8 * (j + 1))
                for k in range(KT):
                    if k >= 2:
                        pe.wait_ge(scaled, KT * j + k - 1)
                    pe.matmul(tr_ps[:, k % 2, :, :], keep["chan_in"][:, k * P:(k + 1) * P], route_t[:, j % 2, :],
                              start=True, stop=True).then_inc(sc_mm, 1)

            def ffn(n):
                j, t = divmod(n, QT)
                tok = slice(t * P, (t + 1) * P)
                if n >= 2:
                    pe.wait_ge(z_mul, n - 1)
                for h in range(2):
                    if 2 * n + h >= 1:
                        pe.wait_ge(osc_sb, 2 * n + h)
                    pe.matmul(osc_ps[:], route_t[:, j % 2, tok], keep["chan_out"][:, h * HALF:(h + 1) * HALF],
                              start=True, stop=True).then_inc(osc_mm, 1)
                    if h == 0:
                        ks = range(0, 4)
                    else:
                        ks = range(4, KT)
                    for k in ks:
                        if t == 0:
                            pe.wait_ge(xs_l, KT * j + k + 1)
                        for part in (xs_hi, xs_lo):
                            for o in range(2):
                                last = pe.matmul(z_ps[n % 2][:, o, :], part[:, k, tok],
                                                 keep["sign_t"][:, k, o * HALF:(o + 1) * HALF],
                                                 start=(k == 0 and part is xs_hi), stop=(k == KT - 1 and part is xs_lo))
                last.then_inc(z_mm, 1)

            for n in range(QT):
                x_transposes(n)
            gate(0)
            route_transposes(0)
            in_scale(0)
            for j in range(BATCH):
                more = j + 1 < BATCH
                ffn(QT * j)
                if more:
                    x_transposes(QT * (j + 1))
                    x_transposes(QT * (j + 1) + 1)
                ffn(QT * j + 1)
                if more:
                    x_transposes(QT * (j + 1) + 2)
                    x_transposes(QT * (j + 1) + 3)
                ffn(QT * j + 2)
                if more:
                    gate(j + 1)
                ffn(QT * j + 3)
                if more:
                    route_transposes(j + 1)
                    in_scale(j + 1)

        @block.scalar
        def _(act):
            def ln_root(n):
                act.wait_ge(ln_var, n + 1)
                act.activation(ln[:, n % 2, 1:2], ln[:, n % 2, 0:1], ACT.Sqrt).then_inc(ln_sqrt, 1)

            def x_high(n):
                j, t = divmod(n, QT)
                if j >= 2 and t == 0:
                    act.wait_ge(xn_out[j % 2], 32)
                    act.wait_ge(summed, KT * (j - 1))
                for b in range(2):
                    act.wait_ge(x_tr, 2 * n + b + 1)
                    act.activation(xn[j % 2][PHI][:, 4 * b:4 * b + 4, t * P:(t + 1) * P], tr_ps[:, b, :, :],
                                   ACT.Copy).then_inc(x_hi, 1)

            def gate_copy(j):
                act.wait_ge(gate_mm, j + 1)
                act.activation(logit_t[:], small_ps[0:2 * EXPERTS, :], ACT.Copy).then_inc(gate_sb, 1)
                act.wait_ge(gate_tr, j + 1)
                act.activation(parts[:].rearrange("p t e -> p (t e)"), small_ps[:, 0:QT * 2 * EXPERTS], ACT.Copy).then_inc(gate_sb, 1)
                act.wait_ge(shifted, j + 1)
                act.activation(route_e[:], route[:], ACT.Exp).then_inc(expd, 1)

            def route_copy(j):
                act.wait_ge(route_tr, j + 1)
                act.activation(route_t[:, j % 2, :], small_ps[:], ACT.Copy).then_inc(route_sb, 1)

            def xs_high(j):
                for k in range(KT):
                    act.wait_ge(scaled, KT * j + k + 1)
                    if j >= 1 and k == 0:
                        act.wait_ge(z_mm, QT * j)
                    act.activation(xs_hi[:, k, :], xs_full[:, k % 2, :], ACT.Copy).then_inc(xs_h, 1)

            def out_scale(n):
                for h in range(2):
                    act.wait_ge(osc_mm, 2 * n + h + 1)
                    if n >= 1 and h == 0:
                        act.wait_ge(z_mul, n)
                    act.activation(out_sc[:, h, :], osc_ps[:], ACT.Copy).then_inc(osc_sb, 1)

            for n in range(QT):
                ln_root(n)
                x_high(n)
            gate_copy(0)
            route_copy(0)
            xs_high(0)
            for j in range(BATCH):
                more = j + 1 < BATCH
                m = QT * (j + 1)
                if more:
                    ln_root(m)
                    ln_root(m + 1)
                out_scale(QT * j)
                if more:
                    x_high(m)
                    x_high(m + 1)
                    ln_root(m + 2)
                    ln_root(m + 3)
                out_scale(QT * j + 1)
                if more:
                    x_high(m + 2)
                    x_high(m + 3)
                out_scale(QT * j + 2)
                if more:
                    gate_copy(j + 1)
                out_scale(QT * j + 3)
                if more:
                    route_copy(j + 1)
                    xs_high(j + 1)

        @block.vector
        def _(dve):
            chain = [0]

            def then(ins):
                chain[0] += 1
                ins.then_inc(ln_a, 1)
                dve.wait_ge(ln_a, chain[0])

            def layer_norm(n):
                b = n % 2
                dve.wait_ge(x_in[b], 16 * (n // 2 + 1))
                for h in range(2):
                    last = dve.bn_stats(stats[:, b, h, :], x_tile[:, b, h * HALF:(h + 1) * HALF])
                then(last)
                then(dve.bn_aggr(moments[:, b, :], stats[:, b, :, :]))
                dve.tensor_scalar(ln[:, b, 0:1], moments[:, b, 1:2], LN_EPS, None, ALU.add).then_inc(ln_var, 1)
                dve.wait_ge(ln_sqrt, n + 1)
                then(dve.reciprocal(ln[:, b, 2:3], ln[:, b, 1:2]))
                then(dve.tensor_tensor(ln[:, b, 3:4], ln[:, b, 2:3], ln[:, b, 2:3], ALU.mult))
                then(dve.tensor_tensor(ln[:, b, 4:5], ln[:, b, 3:4], ln[:, b, 0:1], ALU.mult))
                then(dve.tensor_scalar(ln[:, b, 5:6], ln[:, b, 4:5], -0.5, 1.5, ALU.mult, ALU.add))
                then(dve.tensor_tensor(ln[:, b, 6:7], ln[:, b, 2:3], ln[:, b, 5:6], ALU.mult))
                dve.tensor_scalar(x_tile[:, b, :], x_tile[:, b, :], moments[:, b, 0:1], ln[:, b, 6:7],
                                  ALU.subtract, ALU.mult).then_inc(normed, 1)

            def x_low(n):
                j, t = divmod(n, QT)
                tok = slice(t * P, (t + 1) * P)
                for b in range(2):
                    dve.wait_ge(x_hi, 2 * n + b + 1)
                    ks = slice(4 * b, 4 * b + 4)
                    dve.tensor_tensor(xn[j % 2][PLO][:, ks, tok], tr_ps[:, b, :, :], raw(xn[j % 2][PHI][:, ks, tok]),
                                      ALU.subtract).then_inc(x_lo, 1)

            def router(j):
                dve.wait_ge(gate_sb, 2 * j + 2)
                then(dve.tensor_tensor(route[:], parts[:, :, 0:EXPERTS], parts[:, :, EXPERTS:2 * EXPERTS], ALU.add))
                then(dve.tensor_reduce(route_m[:, 0, :], route[:], AX.X, ALU.max))
                dve.tensor_tensor(route[:], route[:], route_m[:, 0, :].unsqueeze(2).to_broadcast([P, QT, EXPERTS]),
                                  ALU.subtract).then_inc(shifted, 1)
                dve.wait_ge(expd, j + 1)
                then(dve.tensor_reduce(route_m[:, 1, :], route_e[:], AX.X, ALU.add))
                then(dve.reciprocal(route_m[:, 2, :], route_m[:, 1, :]))
                then(dve.tensor_tensor(route[:], route_e[:], route_m[:, 2, :].unsqueeze(2).to_broadcast([P, QT, EXPERTS]), ALU.mult))
                if j >= 1:
                    dve.wait_ge(route_tr, j)
                else:
                    dve.wait_ge(zeroed, 1)
                dve.tensor_copy(route4[:, :, 0:EXPERTS], route[:])
                then(dve.tensor_copy(route4[:, :, 32:32 + EXPERTS], route[:]))
                for c in (64, 96):
                    dve.tensor_tensor(route4[:, :, c:c + EXPERTS], route[:], raw(route4[:, :, 0:EXPERTS]),
                                      ALU.subtract).then_inc(route_ok, 1)

            def scale(j):
                for k in range(KT):
                    dve.wait_ge(sc_mm, KT * j + k + 1)
                    dve.wait_ge(summed, KT * j + k + 1)
                    if KT * j + k >= 2:
                        dve.wait_ge(xs_l, KT * j + k - 1)
                    dve.tensor_tensor(xs_full[:, k % 2, :], tr_ps[:, k % 2, :, :].rearrange("p a b -> p (a b)"),
                                      xn_sum[:, k % 2, :], ALU.mult).then_inc(scaled, 1)

            def z_scale(n):
                dve.wait_ge(z_mm, n + 1)
                dve.wait_ge(osc_sb, 2 * n + 2)
                if n >= 2:
                    dve.wait_ge(z_out[n % 2], 16 * (n // 2))
                dve.tensor_tensor(z[:, n % 2, :].rearrange("p (a b) -> p a b", a=2), z_ps[n % 2][:], out_sc[:],
                                  ALU.mult).then_inc(z_mul, 1)

            layer_norm(0)
            for n in range(1, QT + 1):
                if n < QT:
                    layer_norm(n) if n < 2 else None
                x_low(n - 1)
                if 2 <= n + 1 < QT:
                    layer_norm(n + 1)
            router(0)
            scale(0)
            for j in range(BATCH):
                more = j + 1 < BATCH
                m = QT * (j + 1)
                if more:
                    layer_norm(m)
                    layer_norm(m + 1)
                z_scale(QT * j)
                if more:
                    x_low(m)
                    x_low(m + 1)
                    layer_norm(m + 2)
                    layer_norm(m + 3)
                z_scale(QT * j + 1)
                if more:
                    x_low(m + 2)
                    x_low(m + 3)
                z_scale(QT * j + 2)
                if more:
                    router(j + 1)
                z_scale(QT * j + 3)
                if more:
                    scale(j + 1)

        @block.gpsimd
        def _(pool):
            def sum_parts(j):
                pool.wait_ge(x_lo, 8 * (j + 1))
                for k in range(KT):
                    if KT * j + k >= 2:
                        pool.wait_ge(scaled, KT * j + k - 1)
                    pool.tensor_tensor(xn_sum[:, k % 2, :], raw(xn[j % 2][PHI][:, k, :]), raw(xn[j % 2][PLO][:, k, :]),
                                       ALU.add).then_inc(summed, 1)
                    if k >= 1:
                        xs_low(j, k - 1)
                xs_low(j, KT - 1)

            def xs_low(j, k):
                pool.wait_ge(xs_h, KT * j + k + 1)
                pool.tensor_tensor(xs_lo[:, k, :], xs_full[:, k % 2, :], raw(xs_hi[:, k, :]), ALU.subtract).then_inc(xs_l, 1)

            def z_bias(n):
                pool.wait_ge(z_mul, n + 1)
                pool.tensor_tensor(z[:, n % 2, :], z[:, n % 2, :], keep["bias"][:], ALU.add).then_inc(z_add, 1)

            pool.memset(raw(route4[:]), 0.0).then_inc(zeroed, 1)
            sum_parts(0)
            for j in range(BATCH):
                for t in range(QT):
                    z_bias(QT * j + t)
                if j + 1 < BATCH:
                    sum_parts(j + 1)


def attention_block(nc, io, keep, xn, xn_store, att_store):
    with ExitStack() as ctx:
        def sb(name, shape, dt):
            return ctx.enter_context(nc.sbuf_tensor(name, shape, dt))

        def psum(name, shape):
            return ctx.enter_context(nc.psum_tensor(name, shape, F32))

        def sem(name):
            return ctx.enter_context(nc.semaphore(name))

        w_raw = [sb(f"at_w_raw{m}", [P, KT, P], F32) for m in range(3)]
        w_hi = [sb(f"at_w_hi{m}", [P, KT, P], F32R) for m in range(3)]
        w_lo = [sb(f"at_w_lo{m}", [P, KT, P], F32R) for m in range(3)]
        rope = sb("at_rope", [P, 4, SEQ], F32)
        swapped = [sb(f"at_swapped{c}", [P, SEQ], F32) for c in range(2)]
        turned = [sb(f"at_turned{c}", [P, SEQ], F32) for c in range(2)]
        rotated = [sb(f"at_rotated{c}", [P, SEQ], F32) for c in range(2)]
        v_t = sb("at_v_t", [P, SEQ], F32)
        q_st = [[sb(f"at_q_st{p}{h}", [P, SEQ], F32R) for h in range(2)] for p in range(2)]
        k_hh = [[sb(f"at_k_hh{p}{h}", [P, SEQ], F32R) for h in range(2)] for p in range(2)]
        k_l0 = [[sb(f"at_k_l0{p}{h}", [P, SEQ], F32R) for h in range(2)] for p in range(2)]
        v_hl = [sb(f"at_v_hl{p}", [P, QT, 4, HEAD_DIM], F32R) for p in range(2)]
        neg_max = [sb(f"at_neg_max{h}", [P, QT], F32) for h in range(2)]
        row_sum = [sb(f"at_row_sum{h}", [P, QT], F32) for h in range(2)]
        inv_sum = [sb(f"at_inv_sum{h}", [P, QT], F32) for h in range(2)]
        prob = [sb(f"at_prob{h}", [P, 1280], F32) for h in range(2)]
        pt_hi = [sb(f"at_pt_hi{h}", [P, 1280], F32R) for h in range(2)]
        pt_lo = [sb(f"at_pt_lo{h}", [P, 1280], F32R) for h in range(2)]
        low_half = sb("at_low_half", [P, SEQ], F32)
        att_t = [sb(f"at_att_t{p}", [P, SEQ], F32) for p in range(2)]

        proj_ps = [psum(f"at_proj{i}", [P, SEQ]) for i in range(2)]
        score_ps = [psum(f"at_score{i}", [P, SEQ]) for i in range(3)]
        pt_ps = [psum(f"at_pt{i}", [P, SEQ]) for i in range(2)]
        out_ps = psum("at_out", [P, SEQ])

        w_in = [sem(f"at_w_in{m}") for m in range(3)]
        w_high, w_ready = sem("at_w_high"), [sem(f"at_w_ready{m}") for m in range(3)]
        rope_in, xn_in, xn_ok = sem("at_rope_in"), sem("at_xn_in"), sem("at_xn_ok")
        zeroed = sem("at_zeroed")
        projected = sem("at_projected")
        rot_read, rot_a, rot_b, rot_done = sem("at_rot_read"), sem("at_rot_a"), sem("at_rot_b"), sem("at_rot_done")
        high_done, qk_ready = sem("at_high_done"), sem("at_qk_ready")
        v_copied, v_tr, v_high, v_ready = sem("at_v_copied"), sem("at_v_tr"), sem("at_v_high"), sem("at_v_ready")
        scored, masked, maxed, expd = sem("at_scored"), sem("at_masked"), sem("at_maxed"), sem("at_expd")
        inverted, normed = sem("at_inverted"), sem("at_normed")
        pt_tr, pt_high, pt_ready = sem("at_pt_tr"), sem("at_pt_high"), sem("at_pt_ready")
        pv_done, half_copied, merged = sem("at_pv_done"), sem("at_half_copied"), sem("at_merged")
        att_out = [sem(f"at_att_out{p}") for p in range(2)]
        block = ctx.enter_context(nc.Block())

        w_dram = [io[w].rearrange("(k p) n -> p k n", p=P) for w in ("wq", "wk", "wv")]
        pair_rows = (slice(0, HEAD_DIM), slice(HEAD_DIM, 2 * HEAD_DIM))
        swap_mask = [i ^ 1 for i in range(32)]

        def loop(engine, step):
            step(0, 0, 0)
            step(0, 1, 1)
            with engine.Fori(1, STEPS // 2) as i:
                step(i, 2 * i, 0)
                step(i, 2 * i + 1, 1)

        @block.sync
        def _(sp):
            sp.dma_start(rope[:], io["rope"].rearrange("c p n -> p c n")).then_inc(rope_in, 16)

            def load_weights(idx, pair):
                for m in range(3):
                    if not isinstance(idx, int) or idx >= 1:
                        sp.wait_ge(w_ready[m], idx)
                    sp.dma_start(w_raw[m][:], w_dram[m][:, :, bass.ts(pair, P)]).then_inc(w_in[m], 16)

            def store(a, parity):
                sp.wait_ge(merged, 2 * a + 2)
                sp.dma_start(att_store[a], att_t[parity][:]).then_inc(att_out[parity], 16)

            sp.sem_inc(xn_ok, 2 * PAIRS)
            load_weights(0, 0)
            load_weights(1, 1)
            store(0, 0)
            with sp.Fori(2, PAIRS) as idx:
                load_weights(idx, idx)
                store(2 * idx - 3, 1)
                store(2 * idx - 2, 0)
            load_weights(PAIRS, 0)
            for b in range(2):
                sp.wait_ge(projected, 3 * (2 * PAIRS - 2 + b) + 3)
                for part in (PHI, PLO):
                    sp.dma_start(raw(xn[b][part][:]), xn_store[b, :, part, :, :]).then_inc(xn_in, 16)
                sp.wait_ge(xn_in, 32 * (b + 1))
                sp.sem_inc(xn_ok, 1 if b == 0 else 2 * PAIRS - 1)
            store(2 * PAIRS - 3, 1)
            store(2 * PAIRS - 2, 0)
            with sp.Fori(PAIRS + 1, 2 * PAIRS) as idx:
                load_weights(idx, idx - PAIRS)
                store(2 * idx - 3, 1)
                store(2 * idx - 2, 0)
            store(STEPS - 3, 1)
            store(STEPS - 2, 0)
            store(STEPS - 1, 1)
            for p in range(2):
                sp.wait_ge(att_out[p], 16 * (STEPS // 2))

        @block.tensor
        def _(pe):
            def project(i, s, b, m, ks=range(KT)):
                bank = (0, 1, 0)[m]
                if ks[0] > 0:
                    pass
                elif b == 0:
                    pe.wait_ge(w_ready[m], i + 1)
                if m == 0:
                    pe.wait_ge(xn_ok, s + 1)
                if m == 2 and ks[0] == 0:
                    pe.wait_ge(rot_read, 2 * s + 1)
                elif m < 2 and later(s, 1):
                    pe.wait_ge((v_copied, v_ready)[m], s)
                hi, lo = xn[b]
                for k in ks:
                    last = split_matmuls(pe, proj_ps[bank][:], (w_hi[m][:, k, :], w_lo[m][:, k, :]), (hi[:, k, :], lo[:, k, :]),
                                         first=(k == 0), final=(k == KT - 1))
                if ks[-1] == KT - 1:
                    last.then_inc(projected, 1)

            def v_transposes(s, b):
                pe.wait_ge(rot_read, 2 * s + 2)
                pe.wait_ge(v_copied, s + 1)
                for t in range(QT):
                    last = pe.transpose(proj_ps[1][:, t * P:(t + 1) * P], v_t[:, t * P:(t + 1) * P], keep["ident"][:])
                last.then_inc(v_tr, 1)

            def scores(a, h, parity):
                n = 2 * a + h
                pe.wait_ge(qk_ready, 2 * a + 2)
                for bank, tiles in enumerate(SCORE_BANKS):
                    if later(n, 1):
                        pe.wait_ge(expd, 3 * (n - 1) + bank + 1)
                    for t, col in tiles:
                        width = (t + 1) * P
                        out = score_ps[bank][:, col:col + width]
                        q = q_st[parity][h][:, t * P:(t + 1) * P]
                        pe.matmul(out, q, k_hh[parity][h][:, 0:width], start=True, stop=False)
                        last = pe.matmul(out, q, k_l0[parity][h][:, 0:width], start=False, stop=True)
                    last.then_inc(scored, 1)

            def prob_transposes(n, h, uses):
                if uses[0] == 0:
                    pe.wait_ge(normed, n + 1)
                for u in uses:
                    tiles = PT_BANKS[u]
                    if u == 2:
                        pe.wait_ge(pt_ready, 3 * n + 1)
                    elif later(n, 1):
                        pe.wait_ge(pt_ready, 3 * n - (0, 1)[u])
                    for kt, col in tiles:
                        for t in range(kt, QT):
                            src = P_COL[t] + kt * P
                            dst = col + (t - kt) * P
                            last = pe.transpose(pt_ps[u % 2][:, dst:dst + P], prob[h][:, src:src + P], keep["ident"][:])
                    last.then_inc(pt_tr, 1)

            def values(a, n, h, parity):
                if h == 0:
                    pe.wait_ge(v_ready, a + 1)
                pe.wait_ge(pt_ready, 3 * n + 3)
                if later(n, 1):
                    pe.wait_ge(merged, n)
                for kt in range(QT):
                    v = v_hl[parity][:, kt, 2 * h:2 * h + 2, :].rearrange("p a d -> p (a d)")
                    cols = slice(PT_COL[kt], PT_COL[kt] + (QT - kt) * P)
                    for part in (pt_hi, pt_lo):
                        last = pe.matmul(out_ps[:, kt * P:SEQ], v, part[h][:, cols], start=(kt == 0 and part is pt_hi),
                                         stop=(kt == QT - 1 and part is pt_lo))
                last.then_inc(pv_done, 1)

            def step(i, s, b):
                project(i, s, b, 0)
                if later(s, 2):
                    values(s - 2, 2 * s - 3, 1, b)
                if later(s, 1):
                    scores(s - 1, 0, 1 - b)
                project(i, s, b, 1)
                if later(s, 1):
                    scores(s - 1, 1, 1 - b)
                    prob_transposes(2 * s - 2, 0, (0, 1))
                project(i, s, b, 2, range(0, KT // 2))
                if later(s, 1):
                    prob_transposes(2 * s - 2, 0, (2,))
                project(i, s, b, 2, range(KT // 2, KT))
                if later(s, 1):
                    prob_transposes(2 * s - 1, 1, (0, 1))
                    values(s - 1, 2 * s - 2, 0, 1 - b)
                v_transposes(s, b)
                if later(s, 1):
                    prob_transposes(2 * s - 1, 1, (2,))

            pe.wait_ge(zeroed, 4)
            loop(pe, step)
            s = STEPS
            values(s - 2, 2 * s - 3, 1, 0)
            scores(s - 1, 0, 1)
            scores(s - 1, 1, 1)
            prob_transposes(2 * s - 2, 0, (0, 1, 2))
            values(s - 1, 2 * s - 2, 0, 1)
            prob_transposes(2 * s - 1, 1, (0, 1, 2))
            values(s - 1, 2 * s - 1, 1, 1)

        @block.scalar
        def _(act):
            def weights_high(idx, m):
                act.wait_ge(w_in[m], 16 * idx + 16)
                if not isinstance(idx, int) or idx >= 1:
                    act.wait_ge(projected, 3 * (2 * idx - 1) + m + 1)
                act.activation(w_hi[m][:], w_raw[m][:], ACT.Copy).then_inc(w_high, 1)

            def rot_high(s, b, c):
                act.wait_ge(rot_done, 2 * s + c + 1)
                if later(s, 2):
                    act.wait_ge(scored, 6 * (s - 1))
                for h, rows in enumerate(pair_rows):
                    if c == 0:
                        last = act.activation(q_st[b][h][rows, :], rotated[0][rows, :], ACT.Copy)
                    else:
                        for dup in pair_rows:
                            last = act.activation(k_hh[b][h][dup, :], rotated[1][rows, :], ACT.Copy)
                last.then_inc(high_done, 1)

            def v_copy(s):
                act.wait_ge(projected, 3 * s + 3)
                if later(s, 1):
                    act.wait_ge(v_tr, s)
                act.activation(v_t[:], proj_ps[0][:], ACT.Copy).then_inc(v_copied, 1)

            def v_hi(a, parity):
                act.wait_ge(v_tr, a + 1)
                if later(a, 2):
                    act.wait_ge(pv_done, 2 * a - 2)
                act.activation(v_hl[parity][:, :, 0:4:3, :], proj_ps[1][:].rearrange("p (t h d) -> p t h d", t=QT, h=2),
                               ACT.Copy).then_inc(v_high, 1)

            def exps(n, h):
                for bank, tiles in enumerate(SCORE_BANKS):
                    act.wait_ge(maxed, 3 * n + bank + 1)
                    if bank == 0 and later(n, 2):
                        act.wait_ge(pt_tr, 3 * n - 3)
                    for t, col in tiles:
                        width = (t + 1) * P
                        last = act.activation(prob[h][:, P_COL[t]:P_COL[t] + width], score_ps[bank][:, col:col + width],
                                              ACT.Exp, bias=neg_max[h][:, t:t + 1], accum_out=row_sum[h][:, t:t + 1])
                    last.then_inc(expd, 1)

            def pt_hi_parts(n, h, uses=(0, 1, 2)):
                for u in uses:
                    act.wait_ge(pt_tr, 3 * n + u + 1)
                    if u == 0 and later(n, 2):
                        act.wait_ge(pv_done, n - 1)
                    act.activation(pt_hi[h][:, 512 * u:512 * u + PT_WIDTH[u]], pt_ps[u % 2][:, 0:PT_WIDTH[u]],
                                   ACT.Copy).then_inc(pt_high, 1)

            def copy_low_half(n, h):
                act.wait_ge(pv_done, n + 1)
                if later(n, 1):
                    act.wait_ge(merged, n)
                act.activation(low_half[pair_rows[h], :], out_ps[pair_rows[1 - h], :], ACT.Copy).then_inc(half_copied, 1)

            def step(i, s, b):
                if later(s, 1):
                    v_hi(s - 1, 1 - b)
                if later(s, 2):
                    copy_low_half(2 * s - 3, 1)
                rot_high(s, b, 0)
                if later(s, 1):
                    exps(2 * s - 2, 0)
                    exps(2 * s - 1, 1)
                    pt_hi_parts(2 * s - 2, 0)
                rot_high(s, b, 1)
                if b == 1:
                    for m in range(2):
                        next_weights(i, m)
                v_copy(s)
                if later(s, 1):
                    pt_hi_parts(2 * s - 1, 1, (0, 1))
                    copy_low_half(2 * s - 2, 0)
                    pt_hi_parts(2 * s - 1, 1, (2,))
                if b == 1:
                    next_weights(i, 2)

            def next_weights(i, m):
                weights_high(i + 1, m)

            for m in range(3):
                weights_high(0, m)
            step(0, 0, 0)
            step(0, 1, 1)
            with act.Fori(1, STEPS // 2 - 1) as i:
                step(i, 2 * i, 0)
                step(i, 2 * i + 1, 1)
            next_weights = lambda i, m: None
            i = STEPS // 2 - 1
            step(i, 2 * i, 0)
            step(i, 2 * i + 1, 1)
            s = STEPS
            v_hi(s - 1, 1)
            copy_low_half(2 * s - 3, 1)
            exps(2 * s - 2, 0)
            exps(2 * s - 1, 1)
            pt_hi_parts(2 * s - 2, 0)
            copy_low_half(2 * s - 2, 0)
            pt_hi_parts(2 * s - 1, 1)
            copy_low_half(2 * s - 1, 1)

        @block.vector
        def _(dve):
            def rotate_read(s, c):
                dve.wait_ge(projected, 3 * s + c + 1)
                if later(s, 1):
                    dve.wait_ge(rot_done, 2 * s + c - 1)
                dve.tensor_tensor(turned[c][:], proj_ps[c][:], rope[:, 2 * c, :], ALU.mult)
                dve.stream_shuffle(swapped[c][:], proj_ps[c][:], swap_mask).then_inc(rot_read, 1)

            def q_low(s, b):
                dve.wait_ge(high_done, 2 * s + 1)
                for h, rows in enumerate(pair_rows):
                    last = dve.tensor_tensor(q_st[b][h][pair_rows[1 - h], :], rotated[0][rows, :], raw(q_st[b][h][rows, :]),
                                             ALU.subtract)
                last.then_inc(qk_ready, 1)

            def k_low(s, b):
                dve.wait_ge(high_done, 2 * s + 2)
                for h, rows in enumerate(pair_rows):
                    last = dve.tensor_tensor(k_l0[b][h][rows, :], rotated[1][rows, :], raw(k_hh[b][h][rows, :]), ALU.subtract)
                last.then_inc(qk_ready, 1)

            def v_low(a, parity):
                dve.wait_ge(v_high, a + 1)
                dve.tensor_tensor(v_hl[parity][:, :, 1:3, :], proj_ps[1][:].rearrange("p (t h d) -> p t h d", t=QT, h=2),
                                  raw(v_hl[parity][:, :, 0:4:3, :]), ALU.subtract).then_inc(v_ready, 1)

            def maxima(n, h):
                for bank, tiles in enumerate(SCORE_BANKS):
                    dve.wait_ge(scored, 3 * n + bank + 1)
                    for t, col in tiles:
                        diag = score_ps[bank][:, col + t * P:col + (t + 1) * P]
                        last = dve.tensor_tensor(diag, diag, keep["causal"][:], ALU.add)
                    last.then_inc(masked, 1)
                    dve.wait_ge(masked, 3 * n + bank + 1)
                    for t, col in tiles:
                        last = dve.tensor_reduce(neg_max[h][:, t:t + 1], score_ps[bank][:, col:col + (t + 1) * P], AX.X,
                                                 ALU.max, negate=True)
                    last.then_inc(maxed, 1)

            def invert(n, h):
                dve.wait_ge(expd, 3 * n + 3)
                if later(n, 2):
                    dve.wait_ge(normed, n - 1)
                dve.reciprocal(inv_sum[h][:], row_sum[h][:]).then_inc(inverted, 1)

            def pt_low_parts(n, h, uses=(0, 1, 2)):
                for u in uses:
                    dve.wait_ge(pt_high, 3 * n + u + 1)
                    cols = slice(512 * u, 512 * u + PT_WIDTH[u])
                    dve.tensor_tensor(pt_lo[h][:, cols], pt_ps[u % 2][:, 0:PT_WIDTH[u]], raw(pt_hi[h][:, cols]),
                                      ALU.subtract).then_inc(pt_ready, 1)

            def merge(a, n, h, parity):
                dve.wait_ge(half_copied, n + 1)
                if h == 0 and later(a, 2):
                    dve.wait_ge(att_out[parity], 16 * ((a - parity) // 2))
                rows = pair_rows[h]
                dve.tensor_tensor(att_t[parity][rows, :], out_ps[rows, :], low_half[rows, :], ALU.add).then_inc(merged, 1)

            def step(i, s, b):
                if later(s, 1):
                    v_low(s - 1, 1 - b)
                rotate_read(s, 0)
                if later(s, 2):
                    merge(s - 2, 2 * s - 3, 1, b)
                if later(s, 1):
                    maxima(2 * s - 2, 0)
                    invert(2 * s - 2, 0)
                q_low(s, b)
                rotate_read(s, 1)
                if later(s, 1):
                    maxima(2 * s - 1, 1)
                    invert(2 * s - 1, 1)
                    pt_low_parts(2 * s - 2, 0)
                k_low(s, b)
                if later(s, 1):
                    pt_low_parts(2 * s - 1, 1, (0, 1))
                    merge(s - 1, 2 * s - 2, 0, 1 - b)
                    pt_low_parts(2 * s - 1, 1, (2,))

            for p in range(2):
                dve.memset(raw(k_l0[p][0][HEAD_DIM:P, :]), 0.0).then_inc(zeroed, 1)
                dve.memset(raw(k_l0[p][1][0:HEAD_DIM, :]), 0.0).then_inc(zeroed, 1)
            dve.wait_ge(rope_in, 16)
            loop(dve, step)
            s = STEPS
            v_low(s - 1, 1)
            merge(s - 2, 2 * s - 3, 1, 0)
            maxima(2 * s - 2, 0)
            invert(2 * s - 2, 0)
            maxima(2 * s - 1, 1)
            invert(2 * s - 1, 1)
            pt_low_parts(2 * s - 2, 0)
            merge(s - 1, 2 * s - 2, 0, 1)
            pt_low_parts(2 * s - 1, 1)
            merge(s - 1, 2 * s - 1, 1, 1)

        @block.gpsimd
        def _(pool):
            def rotate(s, c):
                pool.wait_ge(rot_read, 2 * s + c + 1)
                pool.tensor_tensor(swapped[c][:], swapped[c][:], rope[:, 2 * c + 1, :], ALU.mult).then_inc(rot_a, 1)
                pool.wait_ge(rot_a, 2 * s + c + 1)
                if later(s, 1):
                    pool.wait_ge(qk_ready, 2 * s + c - 1)
                pool.tensor_tensor(rotated[c][:], swapped[c][:], turned[c][:], ALU.add).then_inc(rot_done, 1)

            def normalise(n, h):
                pool.wait_ge(inverted, n + 1)
                first = prob[h][:, P_COL[0]:P_COL[0] + P]
                pool.tensor_tensor(first, first, inv_sum[h][:, 0:1].to_broadcast([P, P]), ALU.mult)
                for t in range(1, QT):
                    part = prob[h][:, P_COL[t]:P_COL[t] + (t + 1) * P]
                    last = pool.tensor_scalar(part, part, inv_sum[h][:, t:t + 1], None, ALU.mult)
                last.then_inc(normed, 1)

            def weights_low(idx, m):
                pool.wait_ge(w_high, 3 * idx + m + 1)
                pool.tensor_tensor(w_lo[m][:], w_raw[m][:], raw(w_hi[m][:]), ALU.subtract).then_inc(w_ready[m], 1)

            def step(i, s, b, more=True):
                rotate(s, 0)
                if later(s, 1):
                    normalise(2 * s - 2, 0)
                rotate(s, 1)
                if later(s, 1):
                    normalise(2 * s - 1, 1)
                if b == 1 and more:
                    for m in range(3):
                        weights_low(i + 1, m)

            for m in range(3):
                weights_low(0, m)
            pool.wait_ge(rope_in, 16)
            step(0, 0, 0)
            step(0, 1, 1)
            with pool.Fori(1, STEPS // 2 - 1) as i:
                step(i, 2 * i, 0)
                step(i, 2 * i + 1, 1)
            i = STEPS // 2 - 1
            step(i, 2 * i, 0)
            step(i, 2 * i + 1, 1, more=False)
            normalise(2 * STEPS - 2, 0)
            normalise(2 * STEPS - 1, 1)


def later(count, least):
    return not isinstance(count, int) or count >= least


def output_block(nc, io, keep, att_store, z_store, out):
    with ExitStack() as ctx:
        def sb(name, shape, dt):
            return ctx.enter_context(nc.sbuf_tensor(name, shape, dt))

        def sem(name):
            return ctx.enter_context(nc.semaphore(name))

        wo_raw = sb("ou_wo_raw", [P, 2, EMBED], F32)
        wo_hi = sb("ou_wo_hi", [P, KT, EMBED], F32R)
        wo_lo = sb("ou_wo_lo", [P, KT, EMBED], F32R)
        att_raw = [sb(f"ou_att_raw{p}", [P, PAIRS, SEQ // 2], F32) for p in range(2)]
        att_hi = [sb(f"ou_att_hi{p}", [P, PAIRS, SEQ // 2], F32R) for p in range(2)]
        att_lo = [sb(f"ou_att_lo{p}", [P, PAIRS, SEQ // 2], F32R) for p in range(2)]
        x_tile = sb("ou_x", [P, 2, EMBED], F32)
        z_tile = sb("ou_z", [P, 2, EMBED], F32)
        y_tile = sb("ou_y", [P, 2, EMBED], F32)
        y_ps = [ctx.enter_context(nc.psum_tensor(f"ou_y_ps{i}", [P, 2, HALF], F32)) for i in range(2)]

        wo_in = [sem(f"ou_wo_in{i}") for i in range(2)]
        wo_high, wo_ready = sem("ou_wo_high"), sem("ou_wo_ready")
        att_in = [sem(f"ou_att_in{p}") for p in range(2)]
        x_in = [sem(f"ou_x_in{p}") for p in range(2)]
        att_high, att_ready, y_mm, silu_done, y_mul, y_add = (sem("ou_att_high"), sem("ou_att_ready"), sem("ou_y_mm"),
                                                       sem("ou_silu"), sem("ou_y_mul"), sem("ou_y_add"))
        y_out = [sem(f"ou_y_out{p}") for p in range(2)]
        block = ctx.enter_context(nc.Block())
        att_view = att_store.rearrange("(f h b) p n -> f b p h n", f=2, h=PAIRS)
        GROUPS = 2 * BATCH

        def load_att(eng, g):
            batch, part = divmod(g, 2)
            src = att_view[1 - batch // 2, batch % 2][:, :, part * 256:(part + 1) * 256]
            if g >= 2:
                eng.wait_ge(att_ready, g - 1)
            eng.dma_start(att_raw[g % 2][:], src).then_inc(att_in[g % 2], 16)

        @block.sync
        def _(sp):
            def load_tiles(n):
                if n >= 2:
                    sp.wait_ge(y_add, n - 1)
                rows = slice(n * P, (n + 1) * P)
                sp.dma_start(x_tile[:, n % 2, :], io["x"][rows, :]).then_inc(x_in[n % 2], 16)
                sp.dma_start(z_tile[:, n % 2, :], z_store[rows, :]).then_inc(x_in[n % 2], 16)

            load_att(sp, 0)
            for k in range(KT):
                if k >= 2:
                    sp.wait_ge(wo_ready, k - 1)
                sp.dma_start(wo_raw[:, k % 2, :], io["wo"][k * P:(k + 1) * P, :]).then_inc(wo_in[k % 2], 16)
            load_att(sp, 1)
            load_tiles(0)
            load_tiles(1)
            for n in range(2 * GROUPS):
                if n + 2 < 2 * GROUPS:
                    if n % 2 == 0 and n // 2 + 2 < GROUPS:
                        load_att(sp, n // 2 + 2)
                sp.wait_ge(y_add, n + 1)
                sp.dma_start(out[n * P:(n + 1) * P, :], y_tile[:, n % 2, :]).then_inc(y_out[n % 2], 16)
                if n + 2 < 2 * GROUPS:
                    load_tiles(n + 2)
            for p in range(2):
                sp.wait_ge(y_out[p], 16 * GROUPS)

        @block.tensor
        def _(pe):
            for n in range(2 * GROUPS):
                g = n // 2
                tok = slice((n % 2) * P, (n % 2 + 1) * P)
                if n % 2 == 0:
                    pe.wait_ge(att_ready, g + 1)
                if n >= 2:
                    pe.wait_ge(y_mul, n - 1)
                for k in range(KT):
                    if n == 0:
                        pe.wait_ge(wo_ready, k + 1)
                    for o in range(2):
                        cols = slice(o * HALF, (o + 1) * HALF)
                        last = split_matmuls(pe, y_ps[n % 2][:, o, :], (att_hi[g % 2][:, k, tok], att_lo[g % 2][:, k, tok]),
                                             (wo_hi[:, k, cols], wo_lo[:, k, cols]), first=(k == 0), final=(k == KT - 1))
                last.then_inc(y_mm, 1)

        @block.scalar
        def _(act):
            def split(g):
                act.wait_ge(att_in[g % 2], 16 * (g // 2 + 1))
                if g >= 2:
                    act.wait_ge(y_mm, 2 * (g - 1))
                act.activation(att_hi[g % 2][:], att_raw[g % 2][:], ACT.Copy).then_inc(att_high, 1)

            split(0)
            for k in range(KT):
                act.wait_ge(wo_in[k % 2], 16 * (k // 2 + 1))
                act.activation(wo_hi[:, k, :], wo_raw[:, k % 2, :], ACT.Copy).then_inc(wo_high, 1)
            split(1)
            for n in range(2 * GROUPS):
                act.wait_ge(x_in[n % 2], 32 * (n // 2 + 1))
                act.activation(z_tile[:, n % 2, :], z_tile[:, n % 2, :], ACT.Silu).then_inc(silu_done, 1)
                if n % 2 == 1 and n // 2 + 2 < GROUPS:
                    split(n // 2 + 2)

        @block.vector
        def _(dve):
            for k in range(KT):
                dve.wait_ge(wo_high, k + 1)
                dve.tensor_tensor(wo_lo[:, k, :], wo_raw[:, k % 2, :], raw(wo_hi[:, k, :]), ALU.subtract).then_inc(wo_ready, 1)
            for n in range(2 * GROUPS):
                dve.wait_ge(y_mm, n + 1)
                dve.wait_ge(silu_done, n + 1)
                if n >= 2:
                    dve.wait_ge(y_out[n % 2], 16 * (n // 2))
                dve.tensor_tensor(y_tile[:, n % 2, :].rearrange("p (a b) -> p a b", a=2), y_ps[n % 2][:],
                                  z_tile[:, n % 2, :].rearrange("p (a b) -> p a b", a=2), ALU.mult).then_inc(y_mul, 1)
                dve.wait_ge(y_mul, n + 1)
                dve.tensor_tensor(y_tile[:, n % 2, :], y_tile[:, n % 2, :], x_tile[:, n % 2, :], ALU.add).then_inc(y_add, 1)

        @block.gpsimd
        def _(pool):
            for g in range(GROUPS):
                pool.wait_ge(att_high, g + 1)
                if g >= 2:
                    pool.wait_ge(y_mm, 2 * (g - 1))
                pool.tensor_tensor(att_lo[g % 2][:], att_raw[g % 2][:], raw(att_hi[g % 2][:]), ALU.subtract).then_inc(att_ready, 1)


def build(nc, x, wq, wk, wv, wo, weight, bias, gate_w, in_scale, out_scale, rope, out):
    io = {"x": x.rearrange("b s e -> (b s) e"), "wq": wq, "wk": wk, "wv": wv, "wo": wo, "weight": weight, "bias": bias,
          "gate_w": gate_w, "in_scale": in_scale, "out_scale": out_scale, "rope": rope}
    xn_store = nc.dram_tensor("xn_store", (2, P, 2, KT, SEQ), F32, kind="Internal").ap()
    z_store = nc.dram_tensor("z_store", (BATCH * SEQ, EMBED), F32, kind="Internal").ap()
    att_store = nc.dram_tensor("att_store", (STEPS, P, SEQ), F32, kind="Internal").ap()
    with ExitStack() as whole:
        def sb(ctx, name, shape, dt):
            return ctx.enter_context(nc.sbuf_tensor(name, shape, dt))

        keep = {"ident": sb(whole, "ident", [P, P], F32), "ident_r": sb(whole, "ident_r", [P, P], F32R),
                "ident_bf": sb(whole, "ident_bf", [P, P], BF16), "causal": sb(whole, "causal", [P, P], F32)}
        with ExitStack() as with_xn:
            xn = [[sb(with_xn, f"xn{b}_{part}", [P, KT, SEQ], F32R) for part in ("hi", "lo")] for b in range(2)]
            with ExitStack() as with_ffn:
                keep["sign_t"] = sb(with_ffn, "sign_t", [P, KT, EMBED], F32R)
                keep["chan_in"] = sb(with_ffn, "chan_in", [P, EMBED], F32R)
                keep["chan_out"] = sb(with_ffn, "chan_out", [P, EMBED], F32R)
                keep["gate_t"] = sb(with_ffn, "gate_t", [P, KT, 2 * EXPERTS], F32R)
                keep["bias"] = sb(with_ffn, "bias", [P, EMBED], F32)
                setup_block(nc, io, keep)
                ffn_block(nc, io, keep, xn, xn_store, z_store)
            attention_block(nc, io, keep, xn, xn_store, att_store)
        output_block(nc, io, keep, att_store, z_store, out.rearrange("b s e -> (b s) e"))


_INS = ['L0_attn_hidden_states', 'L0_attn_Wq', 'L0_attn_Wk', 'L0_attn_Wv', 'L0_attn_Wo', 'L0_ffn_weight', 'L0_ffn_bias',
        'L0_ffn_gate_w', 'L0_ffn_in_channel_scale', 'L0_ffn_out_channel_scale']


def rope_table():
    import numpy as np
    inv_freq = (np.float32(1.0) / np.float32(10000.0) ** (np.arange(0, HEAD_DIM, 2, dtype=np.float32) / np.float32(HEAD_DIM))).astype(np.float32)
    angle = (np.arange(SEQ, dtype=np.float32)[None, :] * inv_freq[:, None]).astype(np.float32)
    angle = np.tile(np.repeat(angle, 2, axis=0), (2, 1))
    cos, sin = np.cos(angle).astype(np.float32), np.sin(angle).astype(np.float32)
    return np.stack([cos * np.float32(0.125), sin * np.float32(0.125), cos, sin]).astype(np.float32)


def kernel(**inputs):
    import numpy as _np
    import concourse.bacc as _bacc
    from concourse import mybir as _mybir
    from concourse.bass_utils import run_bass_kernel_spmd as _run

    nc = _bacc.Bacc("TRN2", target_bir_lowering=False, num_devices=1)
    arrays, args = {}, []
    for name in _INS:
        a = _np.ascontiguousarray(inputs[name])
        arrays[f"in_{name}_dram"] = a
        args.append(nc.dram_tensor(f"in_{name}_dram", a.shape, _mybir.dt.from_np(a.dtype), kind="ExternalInput").ap())
    rope = rope_table()
    arrays["in_rope_dram"] = rope
    args.append(nc.dram_tensor("in_rope_dram", rope.shape, _mybir.dt.float32, kind="ExternalInput").ap())
    args.append(nc.dram_tensor("out_0_dram", (BATCH, SEQ, EMBED), _mybir.dt.float32, kind="ExternalOutput").ap())
    build(nc, *args)
    r = _run(nc, [arrays], core_ids=[0])
    return r.results[0]["out_0_dram"]
```

```python
from contextlib import ExitStack

import concourse.bass as bass
from concourse import mybir

F32 = mybir.dt.float32
F32R = mybir.dt.float32r
BF16 = mybir.dt.bfloat16
ALU = mybir.AluOpType
ACT = mybir.ActivationFunctionType
AX = mybir.AxisListType

P = 128
BATCH, SEQ, EMBED = 4, 512, 1024
KT = EMBED // P
QT = SEQ // P
HEADS, HEAD_DIM = 16, 64
PAIRS = HEADS // 2
EXPERTS = 8
HALF = EMBED // 2
LN_EPS = 1e-5
STEPS = 2 * 2 * PAIRS
MASK = -1.0e9 / 8.0
PHI, PLO = 0, 1

SCORE_BANKS = (((3, 0),), ((2, 0), (0, 384)), ((1, 0),))
PT_BANKS = (((0, 0),), ((1, 0), (3, 384)), ((2, 0),))
PT_WIDTH = (512, 512, 256)
P_COL = {3: 0, 2: 512, 0: 896, 1: 1024}
PT_COL = {0: 0, 1: 512, 3: 896, 2: 1024}


def raw(ap):
    return ap.bitcast(F32)


def split_matmuls(pe, out, hi_lo_stationary, hi_lo_moving, first=True, final=True):
    (sh, sl), (mh, ml) = hi_lo_stationary, hi_lo_moving
    pe.matmul(out, sh, mh, start=first, stop=False)
    pe.matmul(out, sh, ml, start=False, stop=False)
    return pe.matmul(out, sl, mh, start=False, stop=final)


def ffn_block(nc, block, io, keep, xn, xn_store, z_store):
    with ExitStack() as ctx:
        def sb(name, shape, dt):
            return ctx.enter_context(nc.sbuf_tensor(name, shape, dt))

        def psum(name, shape, dt=F32):
            return ctx.enter_context(nc.psum_tensor(name, shape, dt))

        sem = keep["sem"]

        x_tiles, xn_full, xs_full = keep["x_tiles"], keep["xn_full"], keep["xs_full"]
        X_SLOT = (0, 1, 2, 5, 0, 1, 2, 5, 3, 4, 0, 1, 2, 5, 3, 4)
        x_slots = [x_tiles[:, i, :] for i in range(3)] + [keep["w_stage"][:, i, :] for i in range(3)]
        x_tile = [x_slots[slot] for slot in X_SLOT]
        stats = sb("ff_stats", [P, 2, 2, 6], F32)
        moments = sb("ff_moments", [P, 2, 2], F32)
        ln = sb("ff_ln", [P, 7, 2], F32)
        logit_t = sb("ff_logit_t", [2 * EXPERTS, SEQ], F32)
        parts = sb("ff_parts", [P, QT, 2 * EXPERTS], F32)
        route = sb("ff_route", [P, QT, EXPERTS], F32)
        route_e = sb("ff_route_e", [P, QT, EXPERTS], F32)
        route_m = sb("ff_route_m", [P, 3, QT], F32)
        route4 = sb("ff_route4", [P, QT, P], F32R)
        route_t = sb("ff_route_t", [P, 2, SEQ], F32R)
        xs_hi = sb("ff_xs_hi", [P, KT, SEQ], F32R)
        xs_lo = sb("ff_xs_lo", [P, KT, SEQ], F32R)
        out_sc = sb("ff_out_sc", [P, 2, HALF], F32)
        z = keep["z"]
        w_rows = keep["w_stage"]
        w_sign = out_sc[:].rearrange("p a b -> p (a b)").bitcast(BF16).rearrange("p (a n) -> p a n", a=2)
        gate_rows = xs_full[0:EXPERTS, :, :].rearrange("p a b -> p (a b)")
        chan_rows = z

        tr_ps = psum("ff_tr", [P, 2, 4, P])
        small_ps = psum("ff_small", [P, SEQ])
        z_ps = [psum(f"ff_z_ps{i}", [P, 2, HALF]) for i in range(2)]
        osc_ps = psum("ff_osc_ps", [P, HALF])
        sign_ps = [z_ps[i][:, 0, :].bitcast(BF16).rearrange("p (k n) -> p k n", k=KT) for i in range(2)]

        def x_bank(n, b):
            return z_ps[b][:, 1, :].rearrange("p (k n) -> p k n", k=4) if n in (1, 3) else tr_ps[:, b, :, :]

        gate_ps = osc_ps[:, 0:KT * EXPERTS].rearrange("p (k e) -> p k e", k=KT)

        w_in = [sem(f"ff_w_in{i}") for i in range(2)]
        bias_in, chan_in_sem, gate_in = sem("ff_bias_in"), sem("ff_chan_in"), sem("ff_gate_in")
        chan_zero, idents, ident_copies = sem("ff_chan_zero"), sem("ff_idents"), sem("ff_ident_copies")
        signed, sign_tr, sign_copied = sem("ff_signed"), sem("ff_sign_tr"), [sem(f"ff_sign_copied{i}") for i in range(2)]
        gate_w_tr, gate_w_hi, chan_hi, tables = sem("ff_gate_w_tr"), sem("ff_gate_w_hi"), sem("ff_chan_hi"), sem("ff_tables")
        chan_lo = sem("ff_chan_lo")
        x_in = [sem(f"ff_x_in{i}") for i in range(6)]
        ln_a, ln_var, ln_sqrt, normed = sem("ff_ln_a"), sem("ff_ln_var"), sem("ff_ln_sqrt"), sem("ff_normed")
        x_tr, x_hi, x_lo, xn_out = sem("ff_x_tr"), sem("ff_x_hi"), sem("ff_x_lo"), [sem(f"ff_xn_out{i}") for i in range(2)]
        gate_mm, gate_sb, gate_tr = sem("ff_gate_mm"), sem("ff_gate_sb"), sem("ff_gate_tr")
        shifted, expd, route_ok, route_tr, route_sb = (sem("ff_shifted"), sem("ff_expd"), sem("ff_route_ok"),
                                                       sem("ff_route_tr"), sem("ff_route_sb"))
        route_zero = sem("ff_route_zero")
        sc_mm, scaled, xs_h, xs_l, xs_free = sem("ff_sc_mm"), sem("ff_scaled"), sem("ff_xs_h"), sem("ff_xs_l"), sem("ff_xs_free")
        z_mm, osc_mm, osc_sb, z_mul, z_add = sem("ff_z_mm"), sem("ff_osc_mm"), sem("ff_osc_sb"), sem("ff_z_mul"), keep["z_add"]
        z_out = keep["z_out"]

        @block.sync
        def _(sp):
            def load(n):
                slot = X_SLOT[n]
                before = [i for i in range(n) if X_SLOT[i] == slot]
                if before:
                    sp.wait_ge(x_tr, 2 * (before[-1] + 1))
                elif slot in (3, 4):
                    sp.wait_ge(signed, KT)
                sp.dma_start(x_tile[n], io["x"][n * P:(n + 1) * P, :]).then_inc(x_in[slot], 16)

            def load_rows(t):
                if t >= 2:
                    sp.wait_ge(signed, t - 1)
                sp.dma_start(w_rows[:, t % 2, :], io["weight"][t * P:(t + 1) * P, :]).then_inc(w_in[t % 2], 16)

            def store_xn(j):
                sp.wait_ge(x_lo, 8 * (j + 1))
                sp.dma_start(xn_store[j, :, 0, :, :], raw(xn[j][PHI][:])).then_inc(xn_out[j], 16)
                sp.dma_start(xn_store[j, :, 1, :, :], raw(xn[j][PLO][:])).then_inc(xn_out[j], 16)

            def store_z(n):
                sp.wait_ge(z_add, n + 1)
                sp.dma_start(z_store[n * P:(n + 1) * P, :], z[:, n % 2, :]).then_inc(z_out[n % 2], 16)

            load(0)
            load(1)
            load_rows(0)
            load(2)
            load(3)
            load_rows(1)
            sp.dma_start(gate_rows, io["gate_w"]).then_inc(gate_in, 16)
            sp.wait_ge(chan_zero, 1)
            for c, table in enumerate((io["in_scale"], io["out_scale"])):
                for r in range(4):
                    sp.dma_start(chan_rows[32 * r:32 * r + EXPERTS, c, :], table).then_inc(chan_in_sem, 16)
            load_rows(2)
            load_rows(3)
            load(4)
            load(5)
            for t in range(4, KT):
                load_rows(t)
            sp.dma_start(keep["bias"][:], io["bias"].rearrange("(a n) -> a n", a=1).to_broadcast([P, EMBED])).then_inc(bias_in, 16)
            for n in range(6, 10):
                load(n)
            sp.sem_inc(keep["xn_ok"], 2 * PAIRS)
            for j in range(BATCH):
                if j < 2:
                    store_xn(j)
                store_z(QT * j)
                for n in ((10,), (14,), (), ())[j]:
                    load(n)
                store_z(QT * j + 1)
                for n in ((11, 12, 13), (15,), (), ())[j]:
                    load(n)
                if j == 2:
                    sp.wait_ge(x_tr, 2 * BATCH * QT)
                    for m, w in enumerate(("wq", "wk", "wv")):
                        rows = w_rows[:, m, :].rearrange("p (k n) -> p k n", k=KT)
                        sp.dma_start(rows, io[w].rearrange("(k p) n -> p k n", p=P)[:, :, 0:P]).then_inc(keep["w_in"][m], 16)
                if j == BATCH - 1:
                    sp.wait_ge(xs_l, BATCH * KT)
                    sp.dma_start(keep["rope"][:], io["rope"].rearrange("c p n -> p c n")).then_inc(keep["rope_in"], 16)
                store_z(QT * j + 2)
                store_z(QT * j + 3)
            for i in range(2):
                sp.wait_ge(xn_out[i], 32)

        @block.tensor
        def _(pe):
            def sign_transposes(t):
                pe.wait_ge(signed, t + 1)
                if t >= 2:
                    pe.wait_ge(sign_copied[t % 2], t // 2)
                for k in range(KT):
                    last = pe.transpose(sign_ps[t % 2][:, k, :], w_sign[:, t % 2, k * P:(k + 1) * P], keep["ident_bf"][:])
                last.then_inc(sign_tr, 1)

            def gate_w_transposes():
                pe.wait_ge(gate_in, 16)
                for k in range(KT):
                    last = pe.transpose(gate_ps[:, k, :], gate_rows[:, k * P:(k + 1) * P], keep["ident"][0:EXPERTS, 0:EXPERTS])
                last.then_inc(gate_w_tr, 1)

            def x_transposes(n):
                pe.wait_ge(normed, n + 1)
                for b in range(2):
                    if n >= QT:
                        pe.wait_ge(x_lo, 2 * (n - 1) + b + 1)
                    elif n >= 2:
                        pe.wait_ge(x_lo, 2 * (n - 2) + b + 1)
                    if n >= QT and n % QT == 0:
                        pe.wait_ge(scaled, KT * (n // QT))
                    for k in range(4):
                        last = pe.transpose(x_bank(n, b)[:, k, :], x_tile[n][:, (4 * b + k) * P:(4 * b + k + 1) * P],
                                            keep["ident"][:])
                    last.then_inc(x_tr, 1)

            def gate(j):
                hi, lo = xn[j % 2]
                pe.wait_ge(x_lo, 8 * (j + 1))
                if j >= 1:
                    pe.wait_ge(route_sb, j)
                for k in range(KT):
                    pe.matmul(small_ps[0:2 * EXPERTS, :], keep["gate_t"][:, k, :], hi[:, k, :], start=(k == 0), stop=False)
                    last = pe.matmul(small_ps[0:2 * EXPERTS, :], keep["gate_t"][:, k, :], lo[:, k, :], start=False, stop=(k == KT - 1))
                last.then_inc(gate_mm, 1)

            def gate_transposes(j):
                pe.wait_ge(gate_sb, 2 * j + 1)
                for t in range(QT):
                    last = pe.transpose(small_ps[:, 16 * t:16 * t + 16], logit_t[:, t * P:(t + 1) * P],
                                        keep["ident"][0:2 * EXPERTS, 0:2 * EXPERTS])
                last.then_inc(gate_tr, 1)

            def route_transposes(j):
                pe.wait_ge(route_ok, 2 * (j + 1))
                for t in range(QT):
                    last = pe.transpose(small_ps[:, t * P:(t + 1) * P].bitcast(F32R), route4[:, t, :], keep["ident_r"][:])
                last.then_inc(route_tr, 1)

            def in_scale(j, k):
                if k == 0:
                    pe.wait_ge(route_sb, j + 1)
                    pe.wait_ge(x_lo, 8 * (j + 1))
                if k >= 2:
                    pe.wait_ge(scaled, KT * j + k - 1)
                pe.matmul(tr_ps[:, k % 2, :, :], keep["chan_in"][:, k * P:(k + 1) * P], route_t[:, j % 2, :],
                          start=True, stop=True).then_inc(sc_mm, 1)

            def ffn(n, ks):
                j, t = divmod(n, QT)
                tok = slice(t * P, (t + 1) * P)
                for k in ks:
                    if k == 0 and n >= 2:
                        pe.wait_ge(z_mul, n - 1)
                    if k % 4 == 0:
                        h = k // 4
                        if 2 * n + h >= 1:
                            pe.wait_ge(osc_sb, 2 * n + h)
                        pe.matmul(osc_ps[:], route_t[:, j % 2, tok], keep["chan_out"][:, h * HALF:(h + 1) * HALF],
                                  start=True, stop=True).then_inc(osc_mm, 1)
                    if t == 0:
                        pe.wait_ge(xs_l, KT * j + k + 1)
                    for part in (xs_hi, xs_lo):
                        for o in range(2):
                            last = pe.matmul(z_ps[n % 2][:, o, :], part[:, k, tok],
                                             keep["sign_t"][:, k, o * HALF:(o + 1) * HALF],
                                             start=(k == 0 and part is xs_hi), stop=(k == KT - 1 and part is xs_lo))
                    if t == QT - 1 and k < KT - 1:
                        last.then_inc(xs_free, 1)
                if ks[-1] == KT - 1:
                    last.then_inc(z_mm, 1)

            pe.wait_ge(ident_copies, 2)
            sign_transposes(0)
            x_transposes(0)
            sign_transposes(1)
            x_transposes(1)
            gate_w_transposes()
            x_transposes(2)
            x_transposes(3)
            sign_transposes(2)
            pe.wait_ge(tables, 1)
            gate(0)
            sign_transposes(3)
            gate_transposes(0)
            sign_transposes(4)
            sign_transposes(5)
            route_transposes(0)
            pe.wait_ge(chan_hi, 2)
            pe.wait_ge(chan_lo, 4)
            in_scale(0, 0)
            in_scale(0, 1)
            sign_transposes(6)
            in_scale(0, 2)
            in_scale(0, 3)
            sign_transposes(7)
            for i in range(2):
                pe.wait_ge(sign_copied[i], KT // 2)
            for j in range(BATCH):
                more = j + 1 < BATCH
                m = QT * (j + 1)
                for k in range(4):
                    in_scale(j, k + 4)
                    ffn(QT * j, (k,))
                ffn(QT * j, range(4, 7))
                if more:
                    x_transposes(m)
                ffn(QT * j, range(7, KT))
                ffn(QT * j + 1, range(4))
                if more:
                    x_transposes(m + 1)
                ffn(QT * j + 1, range(4, KT))
                if more:
                    x_transposes(m + 2)
                ffn(QT * j + 2, range(1))
                if more:
                    x_transposes(m + 3)
                ffn(QT * j + 2, range(1, 4))
                if more:
                    gate(j + 1)
                ffn(QT * j + 2, range(4, 6))
                if more:
                    gate_transposes(j + 1)
                ffn(QT * j + 2, range(6, KT))
                ffn(QT * j + 3, range(4))
                if more:
                    route_transposes(j + 1)
                for k in range(4, KT):
                    ffn(QT * j + 3, (k,))
                    if more:
                        in_scale(j + 1, k - 4)

        @block.scalar
        def _(act):
            def sign(t):
                act.wait_ge(w_in[t % 2], 16 * (t // 2 + 1))
                if t >= 2:
                    act.wait_ge(sign_tr, t - 1)
                act.activation(w_sign[:, t % 2, :], w_rows[:, t % 2, :], ACT.Sign).then_inc(signed, 1)

            def sign_copy(t):
                act.wait_ge(sign_tr, t + 1)
                act.activation(keep["sign_t"][:, :, t * P:(t + 1) * P], sign_ps[t % 2], ACT.Copy).then_inc(sign_copied[0], 1)

            def gate_w_high():
                act.wait_ge(gate_w_tr, 1)
                act.activation(keep["gate_t"][:, :, 0:EXPERTS], gate_ps, ACT.Copy).then_inc(gate_w_hi, 1)

            def chan_high(c):
                act.wait_ge(chan_in_sem, 8 * 16)
                act.activation(keep[("chan_in", "chan_out")[c]][:], chan_rows[:, c, :], ACT.Copy).then_inc(chan_hi, 1)

            def ln_root(n):
                act.wait_ge(ln_var, n // 2 + 1)
                act.activation(ln[:, 1, :], ln[:, 0, :], ACT.Sqrt).then_inc(ln_sqrt, 1)

            def x_high(n):
                j, t = divmod(n, QT)
                tok = slice(t * P, (t + 1) * P)
                if j >= 2 and t == 0:
                    act.wait_ge(xn_out[j % 2], 32)
                    act.wait_ge(gate_mm, j - 1)
                for b in range(2):
                    ks = slice(4 * b, 4 * b + 4)
                    act.wait_ge(x_tr, 2 * n + b + 1)
                    act.activation(xn[j % 2][PHI][:, ks, tok], x_bank(n, b), ACT.Copy)
                    if j >= 1 and t == 0:
                        act.wait_ge(scaled, KT * j)
                    act.activation(xn_full[:, ks, tok], x_bank(n, b), ACT.Copy).then_inc(x_hi, 1)

            def gate_copy(j):
                act.wait_ge(gate_mm, j + 1)
                act.activation(logit_t[:], small_ps[0:2 * EXPERTS, :], ACT.Copy).then_inc(gate_sb, 1)

            def parts_copy(j):
                act.wait_ge(gate_tr, j + 1)
                act.activation(parts[:].rearrange("p t e -> p (t e)"), small_ps[:, 0:QT * 2 * EXPERTS], ACT.Copy).then_inc(gate_sb, 1)
                act.wait_ge(shifted, j + 1)
                act.activation(route_e[:], route[:], ACT.Exp).then_inc(expd, 1)

            def route_copy(j):
                act.wait_ge(route_tr, j + 1)
                act.activation(route_t[:, j % 2, :], small_ps[:], ACT.Copy).then_inc(route_sb, 1)

            def xs_high(j, ks):
                for k in ks:
                    act.wait_ge(scaled, KT * j + k + 1)
                    if j >= 1:
                        if k < KT - 1:
                            act.wait_ge(xs_free, (KT - 1) * (j - 1) + k + 1)
                        else:
                            act.wait_ge(z_mm, QT * j)
                    act.activation(xs_hi[:, k, :], xs_full[:, k % 2, :], ACT.Copy).then_inc(xs_h, 1)

            def out_scale(n, h):
                act.wait_ge(osc_mm, 2 * n + h + 1)
                if n >= 1 and h == 0:
                    act.wait_ge(z_mul, n)
                act.activation(out_sc[:, h, :], osc_ps[:], ACT.Copy).then_inc(osc_sb, 1)

            ln_root(0)
            sign(0)
            sign(1)
            x_high(0)
            ln_root(2)
            x_high(1)
            sign_copy(0)
            gate_w_high()
            sign(2)
            x_high(2)
            x_high(3)
            chan_high(0)
            chan_high(1)
            sign_copy(2)
            sign(3)
            ln_root(4)
            gate_copy(0)
            sign(4)
            sign(5)
            parts_copy(0)
            sign_copy(4)
            sign(6)
            route_copy(0)
            sign(7)
            sign_copy(6)
            xs_high(0, range(4))
            for j in range(BATCH):
                more = j + 1 < BATCH
                n = QT * j
                m = n + QT
                out_scale(n, 0)
                xs_high(j, range(4, KT))
                out_scale(n, 1)
                if not more:
                    act.wait_ge(scaled, BATCH * KT)
                    act.wait_ge(x_tr, 2 * BATCH * QT)
                    for m in range(3):
                        act.wait_ge(keep["w_in"][m], 16)
                        act.activation(keep["w_hi"][m][:].rearrange("p k n -> p (k n)"), w_rows[:, m, :], ACT.Copy)\
                           .then_inc(keep["w_high"], 1)
                if more:
                    x_high(m)
                out_scale(n + 1, 0)
                if more:
                    ln_root(m + 2)
                    x_high(m + 1)
                out_scale(n + 1, 1)
                if more:
                    x_high(m + 2)
                out_scale(n + 2, 0)
                if more:
                    x_high(m + 3)
                if m + 4 < BATCH * QT:
                    ln_root(m + 4)
                if more:
                    gate_copy(j + 1)
                out_scale(n + 2, 1)
                if more:
                    parts_copy(j + 1)
                out_scale(n + 3, 0)
                if more:
                    route_copy(j + 1)
                out_scale(n + 3, 1)
                if more:
                    xs_high(j + 1, range(4))

        @block.vector
        def _(dve):
            chain = [0]

            def then(ins):
                chain[0] += 1
                ins.then_inc(ln_a, 1)
                dve.wait_ge(ln_a, chain[0])

            def sign_copy(t):
                dve.wait_ge(sign_tr, t + 1)
                dve.tensor_copy(keep["sign_t"][:, :, t * P:(t + 1) * P], sign_ps[t % 2]).then_inc(sign_copied[1], 1)

            def gate_w_low():
                dve.wait_ge(gate_w_hi, 1)
                dve.tensor_tensor(keep["gate_t"][:, :, EXPERTS:2 * EXPERTS], gate_ps,
                                  raw(keep["gate_t"][:, :, 0:EXPERTS]), ALU.subtract).then_inc(tables, 1)

            def layer_norm(n):
                for t in range(2):
                    slot = X_SLOT[n + t]
                    dve.wait_ge(x_in[slot], 16 * X_SLOT[:n + t + 1].count(slot))
                    for h in range(2):
                        last = dve.bn_stats(stats[:, t, h, :], x_tile[n + t][:, h * HALF:(h + 1) * HALF])
                then(last)
                for t in range(2):
                    last = dve.bn_aggr(moments[:, t, :], stats[:, t, :, :])
                then(last)
                dve.tensor_scalar(ln[:, 0, :], moments[:, :, 1], LN_EPS, None, ALU.add).then_inc(ln_var, 1)
                dve.wait_ge(ln_sqrt, n // 2 + 1)
                then(dve.reciprocal(ln[:, 2, :], ln[:, 1, :]))
                then(dve.tensor_tensor(ln[:, 3, :], ln[:, 2, :], ln[:, 2, :], ALU.mult))
                then(dve.tensor_tensor(ln[:, 4, :], ln[:, 3, :], ln[:, 0, :], ALU.mult))
                then(dve.tensor_scalar(ln[:, 5, :], ln[:, 4, :], -0.5, 1.5, ALU.mult, ALU.add))
                then(dve.tensor_tensor(ln[:, 6, :], ln[:, 2, :], ln[:, 5, :], ALU.mult))
                for t in range(2):
                    dve.tensor_scalar(x_tile[n + t], x_tile[n + t], moments[:, t, 0:1], ln[:, 6, t:t + 1],
                                      ALU.subtract, ALU.mult).then_inc(normed, 1)

            def x_low(n):
                j, t = divmod(n, QT)
                tok = slice(t * P, (t + 1) * P)
                for b in range(2):
                    dve.wait_ge(x_hi, 2 * n + b + 1)
                    ks = slice(4 * b, 4 * b + 4)
                    dve.tensor_tensor(xn[j % 2][PLO][:, ks, tok], x_bank(n, b), raw(xn[j % 2][PHI][:, ks, tok]),
                                      ALU.subtract).then_inc(x_lo, 1)

            def router(j):
                dve.wait_ge(gate_sb, 2 * j + 2)
                then(dve.tensor_tensor(route[:], parts[:, :, 0:EXPERTS], parts[:, :, EXPERTS:2 * EXPERTS], ALU.add))
                then(dve.tensor_reduce(route_m[:, 0, :], route[:], AX.X, ALU.max))
                dve.tensor_tensor(route[:], route[:], route_m[:, 0, :].unsqueeze(2).to_broadcast([P, QT, EXPERTS]),
                                  ALU.subtract).then_inc(shifted, 1)
                dve.wait_ge(expd, j + 1)
                then(dve.tensor_reduce(route_m[:, 1, :], route_e[:], AX.X, ALU.add))
                then(dve.reciprocal(route_m[:, 2, :], route_m[:, 1, :]))
                then(dve.tensor_tensor(route[:], route_e[:], route_m[:, 2, :].unsqueeze(2).to_broadcast([P, QT, EXPERTS]), ALU.mult))
                if j >= 1:
                    dve.wait_ge(route_tr, j)
                else:
                    dve.wait_ge(route_zero, 1)
                dve.tensor_copy(route4[:, :, 0:EXPERTS], route[:])
                then(dve.tensor_copy(route4[:, :, 32:32 + EXPERTS], route[:]))
                for c in (64, 96):
                    dve.tensor_tensor(route4[:, :, c:c + EXPERTS], route[:], raw(route4[:, :, 0:EXPERTS]),
                                      ALU.subtract).then_inc(route_ok, 1)

            def scale(j, ks):
                for k in ks:
                    dve.wait_ge(sc_mm, KT * j + k + 1)
                    if KT * j + k >= 2:
                        dve.wait_ge(xs_l, KT * j + k - 1)
                    dve.tensor_tensor(xs_full[:, k % 2, :], tr_ps[:, k % 2, :, :].rearrange("p a b -> p (a b)"),
                                      xn_full[:, k, :], ALU.mult).then_inc(scaled, 1)

            def z_scale(n):
                dve.wait_ge(z_mm, n + 1)
                dve.wait_ge(osc_sb, 2 * n + 2)
                if n >= 2:
                    dve.wait_ge(z_out[n % 2], 16 * (n // 2))
                dve.tensor_tensor(z[:, n % 2, :].rearrange("p (a b) -> p a b", a=2), z_ps[n % 2][:], out_sc[:],
                                  ALU.mult).then_inc(z_mul, 1)

            dve.wait_ge(idents, 2)
            dve.tensor_copy(keep["ident_r"][:], keep["ident"][:]).then_inc(ident_copies, 1)
            dve.tensor_copy(keep["ident_bf"][:], keep["ident"][:]).then_inc(ident_copies, 1)
            layer_norm(0)
            layer_norm(2)
            x_low(0)
            x_low(1)
            sign_copy(1)
            gate_w_low()
            x_low(2)
            x_low(3)
            layer_norm(4)
            sign_copy(3)
            router(0)
            scale(0, range(2))
            sign_copy(5)
            sign_copy(7)
            scale(0, range(2, 4))
            for j in range(BATCH):
                more = j + 1 < BATCH
                n = QT * j
                m = n + QT
                scale(j, range(4, KT))
                if more:
                    x_low(m)
                z_scale(n)
                if more:
                    layer_norm(m + 2)
                    x_low(m + 1)
                z_scale(n + 1)
                if more:
                    x_low(m + 2)
                    x_low(m + 3)
                if m + 4 < BATCH * QT:
                    layer_norm(m + 4)
                if more:
                    router(j + 1)
                z_scale(n + 2)
                if more:
                    scale(j + 1, range(4))
                z_scale(n + 3)

        @block.gpsimd
        def _(pool):
            def xs_low(j, ks):
                for k in ks:
                    pool.wait_ge(xs_h, KT * j + k + 1)
                    pool.tensor_tensor(xs_lo[:, k, :], xs_full[:, k % 2, :], raw(xs_hi[:, k, :]), ALU.subtract).then_inc(xs_l, 1)

            def chan_low(c):
                name = ("chan_in", "chan_out")[c]
                pool.wait_ge(chan_hi, c + 1)
                for r in (1, 3):
                    rows = slice(32 * r, 32 * r + 32)
                    pool.tensor_tensor(keep[name][rows, :], chan_rows[rows, c, :], raw(keep[name][rows, :]),
                                      ALU.subtract).then_inc(chan_lo, 1)

            def z_bias(n):
                pool.wait_ge(z_mul, n + 1)
                pool.tensor_tensor(z[:, n % 2, :], z[:, n % 2, :], keep["bias"][:], ALU.add).then_inc(z_add, 1)

            pool.memset(keep["ident"][:], 0.0).then_inc(idents, 1)
            pool.wait_ge(idents, 1)
            pool.affine_select(out=keep["ident"][:], in_=keep["ident"][:], compare_op=ALU.not_equal, fill=1.0,
                               base=0, pattern=[[-1, P]], channel_multiplier=1).then_inc(idents, 1)
            pool.memset(chan_rows[:], 0.0).then_inc(chan_zero, 1)
            pool.memset(raw(route4[:]), 0.0).then_inc(route_zero, 1)
            pool.memset(keep["causal"][:], 0.0).then_inc(idents, 1)
            pool.wait_ge(idents, 3)
            pool.affine_select(out=keep["causal"][:], in_=keep["causal"][:], compare_op=ALU.is_ge, fill=MASK,
                               base=0, pattern=[[-1, P]], channel_multiplier=1).then_inc(idents, 1)
            pool.wait_ge(idents, 4)
            chan_low(0)
            chan_low(1)
            xs_low(0, range(4))
            pool.wait_ge(bias_in, 16)
            for j in range(BATCH):
                n = QT * j
                xs_low(j, range(4, KT))
                if j >= 1:
                    z_bias(n - 1)
                for t in range(3):
                    z_bias(n + t)
                    if j == BATCH - 1:
                        pool.wait_ge(keep["w_high"], t + 1)
                        pool.tensor_tensor(keep["w_lo"][t][:].rearrange("p k n -> p (k n)"), w_rows[:, t, :],
                                           raw(keep["w_hi"][t][:]).rearrange("p k n -> p (k n)"), ALU.subtract)\
                            .then_inc(keep["w_ready"][t], 1)
                if j + 1 < BATCH:
                    xs_low(j + 1, range(4))
                else:
                    z_bias(n + 3)


def attention_block(nc, block, io, keep, xn, xn_store, z_store, att_store, out):
    with ExitStack() as ctx:
        def sb(name, shape, dt):
            return ctx.enter_context(nc.sbuf_tensor(name, shape, dt))

        def psum(name, shape):
            return ctx.enter_context(nc.psum_tensor(name, shape, F32))

        sem = keep["sem"]

        w_raw = [keep["w_stage"][:, m, :].rearrange("p (k n) -> p k n", k=KT) for m in range(3)]
        w_hi, w_lo = keep["w_hi"], keep["w_lo"]
        rope = keep["rope"]
        turning = sb("at_turning", [P, 2, 2, SEQ], F32)
        swapped = [turning[:, 0, c, :] for c in range(2)]
        turned = [turning[:, 1, c, :] for c in range(2)]
        rotated = [sb(f"at_rotated{c}", [P, SEQ], F32) for c in range(2)]
        v_t = sb("at_v_t", [P, SEQ], F32)
        qk = sb("at_qk", [P, 2, 6, SEQ], F32R)
        q_st, k_hh, k_l0 = ([[qk[:, p, c + h, :] for h in range(2)] for p in range(2)] for c in (0, 2, 4))
        v_hl = [sb(f"at_v_hl{p}", [P, QT, 4, HEAD_DIM], F32R) for p in range(2)]
        neg_max = [sb(f"at_neg_max{h}", [P, QT], F32) for h in range(2)]
        row_sum = [sb(f"at_row_sum{h}", [P, QT], F32) for h in range(2)]
        inv_sum = [sb(f"at_inv_sum{h}", [P, QT], F32) for h in range(2)]
        prob = [sb(f"at_prob{h}", [P, 1280], F32) for h in range(2)]
        pt_hi = [sb(f"at_pt_hi{h}", [P, 1280], F32R) for h in range(2)]
        pt_lo = [sb(f"at_pt_lo{h}", [P, 1280], F32R) for h in range(2)]
        low_half = sb("at_low_half", [P, SEQ], F32)
        att_t = [sb(f"at_att_t{p}", [P, SEQ], F32) for p in range(2)]

        wo_raw = keep["w_stage"]
        wo_part = [[xn[k // 4][part][:].rearrange("p k n -> p (k n)")[:, (k % 4) * EMBED:(k % 4 + 1) * EMBED]
                    for part in (PHI, PLO)] for k in range(KT)]
        att_raw = rope[:].rearrange("p (a b) n -> p a (b n)", a=2)
        x_tile = keep["z"]
        z_tile = turning[:].rearrange("p a b n -> p a (b n)")
        y_tile = [prob[p][:, 0:EMBED] for p in range(2)]

        proj_ps = [psum(f"at_proj{i}", [P, SEQ]) for i in range(2)]
        score_ps = [psum(f"at_score{i}", [P, SEQ]) for i in range(3)]
        pt_ps = [psum(f"at_pt{i}", [P, SEQ]) for i in range(2)]
        out_ps = psum("at_out", [P, SEQ])
        y_ps = [proj_ps, score_ps[0:2]]

        w_in = keep["w_in"]
        w_high, w_ready, rope_in = keep["w_high"], keep["w_ready"], keep["rope_in"]
        xn_in, xn_ok = sem("at_xn_in"), keep["xn_ok"]
        zeroed = sem("at_zeroed")
        projected = sem("at_projected")
        rot_read, rot_a, rot_done = sem("at_rot_read"), sem("at_rot_a"), sem("at_rot_done")
        high_done, qk_ready = sem("at_high_done"), sem("at_qk_ready")
        v_copied, v_tr, v_high, v_ready = sem("at_v_copied"), sem("at_v_tr"), sem("at_v_high"), sem("at_v_ready")
        scored, masked, maxed, expd = sem("at_scored"), sem("at_masked"), sem("at_maxed"), sem("at_expd")
        inverted, normed = sem("at_inverted"), sem("at_normed")
        pt_tr, pt_high, pt_ready = sem("at_pt_tr"), sem("at_pt_high"), sem("at_pt_ready")
        pv_done, half_copied, merged = sem("at_pv_done"), sem("at_half_copied"), sem("at_merged")
        att_out = [sem(f"at_att_out{p}") for p in range(2)]
        wo_in, wo_high = [sem(f"at_wo_in{i}") for i in range(3)], sem("at_wo_high")
        wo_low_pool, wo_low_dve = sem("at_wo_low_pool"), sem("at_wo_low_dve")
        att_in, xz_in = [sem(f"at_att_in{p}") for p in range(2)], [sem(f"at_xz_in{p}") for p in range(2)]
        att_high, att_split, y_mm = sem("at_att_high"), sem("at_att_split"), sem("at_y_mm")
        silu_done, y_mul, y_add = sem("at_silu_done"), sem("at_y_mul"), sem("at_y_add")
        y_out = [sem(f"at_y_out{p}") for p in range(2)]

        w_dram = [io[w].rearrange("(k p) n -> p k n", p=P) for w in ("wq", "wk", "wv")]
        pair_rows = (slice(0, HEAD_DIM), slice(HEAD_DIM, 2 * HEAD_DIM))
        swap_mask = [i ^ 1 for i in range(32)]

        WO_ON_DVE = (2, 3, 5, 7)
        TILES = BATCH * QT

        def wait_wo(engine, k):
            if k in WO_ON_DVE:
                engine.wait_ge(wo_low_dve, WO_ON_DVE.index(k) + 1)
            else:
                engine.wait_ge(wo_low_pool, k + 1 - sum(d < k for d in WO_ON_DVE))

        def loop(engine, step):
            step(0, 0, 0)
            step(0, 1, 1)
            with engine.Fori(1, STEPS // 2) as i:
                step(i, 2 * i, 0)
                step(i, 2 * i + 1, 1)

        @block.sync
        def _(sp):
            def load_weights(idx, pair):
                for m in range(3):
                    if not isinstance(idx, int) or idx >= 1:
                        sp.wait_ge(w_ready[m], idx)
                    sp.dma_start(w_raw[m], w_dram[m][:, :, bass.ts(pair, P)]).then_inc(w_in[m], 16)

            def store(a, parity):
                sp.wait_ge(merged, 2 * a + 2)
                sp.dma_start(att_store[a], att_t[parity][:]).then_inc(att_out[parity], 16)

            load_weights(1, 1)
            store(0, 0)
            with sp.Fori(2, PAIRS) as idx:
                load_weights(idx, idx)
                store(2 * idx - 3, 1)
                store(2 * idx - 2, 0)
            load_weights(PAIRS, 0)
            for b in range(2):
                sp.wait_ge(projected, 3 * (2 * PAIRS - 2 + b) + 3)
                for part in (PHI, PLO):
                    sp.dma_start(raw(xn[b][part][:]), xn_store[b, :, part, :, :]).then_inc(xn_in, 16)
                sp.wait_ge(xn_in, 32 * (b + 1))
                sp.sem_inc(xn_ok, 1 if b == 0 else 2 * PAIRS - 1)
            store(2 * PAIRS - 3, 1)
            store(2 * PAIRS - 2, 0)
            with sp.Fori(PAIRS + 1, 2 * PAIRS) as idx:
                load_weights(idx, idx - PAIRS)
                store(2 * idx - 3, 1)
                store(2 * idx - 2, 0)

            def load_wo(k):
                if k < 3:
                    sp.wait_ge(w_ready[k], 2 * PAIRS)
                else:
                    wait_wo(sp, k - 3)
                sp.dma_start(wo_raw[:, k % 3, :], io["wo"][k * P:(k + 1) * P, :]).then_inc(wo_in[k % 3], 16)

            att_view = att_store.rearrange("(f h b) p n -> f b p h n", f=2, h=PAIRS)

            def load_att(n):
                half, b = divmod(n // QT, 2)
                if n % (TILES // 2) == 0:
                    for p in range(2):
                        sp.wait_ge(att_out[p], 16 * PAIRS * (half + 1))
                if n >= 2:
                    sp.wait_ge(att_split, n - 1)
                tok = slice((n % QT) * P, (n % QT + 1) * P)
                sp.dma_start(att_raw[:, n % 2, :].rearrange("p (h n) -> p h n", h=PAIRS), att_view[half, b][:, :, tok])\
                  .then_inc(att_in[n % 2], 16)

            def tile_rows(n):
                m = (n + TILES // 2) % TILES
                return slice(m * P, (m + 1) * P)

            def load_xz(n):
                if n >= 2:
                    sp.wait_ge(y_add, n - 1)
                sp.dma_start(x_tile[:, n % 2, :], io["x"][tile_rows(n), :]).then_inc(xz_in[n % 2], 16)
                sp.dma_start(z_tile[:, n % 2, :], z_store[tile_rows(n), :]).then_inc(xz_in[n % 2], 16)

            for k in range(3):
                load_wo(k)
            store(STEPS - 3, 1)
            sp.wait_ge(rot_done, 2 * STEPS - 1)
            load_att(0)
            load_wo(3)
            sp.wait_ge(rot_done, 2 * STEPS)
            load_att(1)
            for p in range(2):
                sp.wait_ge(keep["z_out"][p], 16 * (TILES // 2))
            load_wo(4)
            load_xz(0)
            load_wo(5)
            load_xz(1)
            load_wo(6)
            load_wo(7)
            store(STEPS - 2, 0)
            store(STEPS - 1, 1)
            for n in range(TILES):
                if n + 2 < TILES:
                    load_att(n + 2)
                sp.wait_ge(y_add, n + 1)
                sp.dma_start(out[tile_rows(n), :], y_tile[n % 2]).then_inc(y_out[n % 2], 16)
                if n + 2 < TILES:
                    load_xz(n + 2)
            for p in range(2):
                sp.wait_ge(y_out[p], 16 * (TILES // 2))

        @block.tensor
        def _(pe):
            def project(i, s, b, m, ks=range(KT)):
                bank = (0, 1, 0)[m]
                if ks[0] == 0:
                    if b == 0:
                        pe.wait_ge(w_ready[m], i + 1)
                    if m == 0:
                        pe.wait_ge(xn_ok, s + 1)
                    if m == 2:
                        pe.wait_ge(rot_read, 2 * s + 1)
                    elif later(s, 1):
                        pe.wait_ge((v_copied, v_ready)[m], s)
                hi, lo = xn[b]
                for k in ks:
                    last = split_matmuls(pe, proj_ps[bank][:], (w_hi[m][:, k, :], w_lo[m][:, k, :]), (hi[:, k, :], lo[:, k, :]),
                                         first=(k == 0), final=(k == KT - 1))
                if ks[-1] == KT - 1:
                    last.then_inc(projected, 1)

            def v_transposes(s):
                pe.wait_ge(rot_read, 2 * s + 2)
                pe.wait_ge(v_copied, s + 1)
                for t in range(QT):
                    last = pe.transpose(proj_ps[1][:, t * P:(t + 1) * P], v_t[:, t * P:(t + 1) * P], keep["ident"][:])
                last.then_inc(v_tr, 1)

            def scores(a, h, parity):
                n = 2 * a + h
                pe.wait_ge(qk_ready, 2 * a + 2)
                if not later(a, 2):
                    pe.wait_ge(zeroed, 4)
                for bank, tiles in enumerate(SCORE_BANKS):
                    if later(n, 1):
                        pe.wait_ge(expd, 3 * (n - 1) + bank + 1)
                    for t, col in tiles:
                        width = (t + 1) * P
                        out = score_ps[bank][:, col:col + width]
                        q = q_st[parity][h][:, t * P:(t + 1) * P]
                        pe.matmul(out, q, k_hh[parity][h][:, 0:width], start=True, stop=False)
                        last = pe.matmul(out, q, k_l0[parity][h][:, 0:width], start=False, stop=True)
                    last.then_inc(scored, 1)

            def prob_transposes(n, h, uses):
                if uses[0] == 0:
                    pe.wait_ge(normed, n + 1)
                for u in uses:
                    tiles = PT_BANKS[u]
                    if u == 2:
                        pe.wait_ge(pt_ready, 3 * n + 1)
                    elif later(n, 1):
                        pe.wait_ge(pt_ready, 3 * n - (0, 1)[u])
                    for kt, col in tiles:
                        for t in range(kt, QT):
                            src = P_COL[t] + kt * P
                            dst = col + (t - kt) * P
                            last = pe.transpose(pt_ps[u % 2][:, dst:dst + P], prob[h][:, src:src + P], keep["ident"][:])
                    last.then_inc(pt_tr, 1)

            def values(a, n, h, parity):
                if h == 0:
                    pe.wait_ge(v_ready, a + 1)
                pe.wait_ge(pt_ready, 3 * n + 3)
                if later(n, 1):
                    pe.wait_ge(merged, n)
                for kt in range(QT):
                    v = v_hl[parity][:, kt, 2 * h:2 * h + 2, :].rearrange("p a d -> p (a d)")
                    cols = slice(PT_COL[kt], PT_COL[kt] + (QT - kt) * P)
                    for part in (pt_hi, pt_lo):
                        last = pe.matmul(out_ps[:, kt * P:SEQ], v, part[h][:, cols], start=(kt == 0 and part is pt_hi),
                                         stop=(kt == QT - 1 and part is pt_lo))
                last.then_inc(pv_done, 1)

            def step(i, s, b):
                project(i, s, b, 0, range(0, KT // 2))
                if later(s, 1):
                    v_transposes(s - 1)
                if later(s, 2):
                    prob_transposes(2 * s - 3, 1, (2,))
                project(i, s, b, 0, range(KT // 2, KT))
                if later(s, 2):
                    values(s - 2, 2 * s - 3, 1, b)
                if later(s, 1):
                    scores(s - 1, 0, 1 - b)
                project(i, s, b, 1)
                if later(s, 1):
                    scores(s - 1, 1, 1 - b)
                    prob_transposes(2 * s - 2, 0, (0, 1))
                project(i, s, b, 2, range(0, KT - 3))
                if later(s, 1):
                    prob_transposes(2 * s - 2, 0, (2,))
                project(i, s, b, 2, range(KT - 3, KT))
                if later(s, 1):
                    values(s - 1, 2 * s - 2, 0, 1 - b)
                    prob_transposes(2 * s - 1, 1, (0, 1))

            loop(pe, step)

            def output(n, p, o, ks, first=False, final=False):
                for k in ks:
                    if first:
                        wait_wo(pe, k)
                    cols = slice(o * HALF, (o + 1) * HALF)
                    last = split_matmuls(pe, y_ps[p][o][:], (w_hi[p][:, k, :], w_lo[p][:, k, :]),
                                         (wo_part[k][PHI][:, cols], wo_part[k][PLO][:, cols]), first=(k == 0), final=(k == KT - 1))
                if o == 1 and ks[-1] == KT - 1:
                    last.then_inc(y_mm, 1)

            s = STEPS
            v_transposes(s - 1)
            prob_transposes(2 * s - 3, 1, (2,))
            pe.wait_ge(att_split, 1)
            output(0, 0, 0, range(0, 3), first=True)
            values(s - 2, 2 * s - 3, 1, 0)
            scores(s - 1, 0, 1)
            output(0, 0, 0, range(3, 4), first=True)
            pe.wait_ge(v_ready, s)
            output(0, 0, 1, range(0, 4))
            scores(s - 1, 1, 1)
            output(0, 0, 0, range(4, 5), first=True)
            prob_transposes(2 * s - 2, 0, (0, 1))
            output(0, 0, 1, range(4, 5))
            prob_transposes(2 * s - 2, 0, (2,))
            values(s - 1, 2 * s - 2, 0, 1)
            prob_transposes(2 * s - 1, 1, (0, 1))
            output(0, 0, 0, range(5, 7), first=True)
            prob_transposes(2 * s - 1, 1, (2,))
            output(0, 0, 1, range(5, 7))
            output(0, 0, 0, range(7, 8), first=True)
            values(s - 1, 2 * s - 1, 1, 1)
            output(0, 0, 1, range(7, 8))
            pe.wait_ge(att_split, 2)
            for o in range(2):
                output(1, 1, o, range(KT))

            def output_tile(n, p):
                pe.wait_ge(att_split, n + 1)
                pe.wait_ge(y_mul, 2 * n - 2)
                for o in range(2):
                    output(n, p, o, range(KT))

            with pe.Fori(1, TILES // 2) as i:
                for p in range(2):
                    output_tile(2 * i + p, p)

        @block.scalar
        def _(act):
            def weights_high(idx, m):
                act.wait_ge(w_in[m], 16 * idx + 16)
                if not isinstance(idx, int) or idx >= 1:
                    act.wait_ge(projected, 3 * (2 * idx - 1) + m + 1)
                act.activation(w_hi[m][:], w_raw[m], ACT.Copy).then_inc(w_high, 1)

            def q_high(s, b):
                act.wait_ge(rot_done, 2 * s + 1)
                if later(s, 2):
                    act.wait_ge(scored, 6 * (s - 1))
                for h, rows in enumerate(pair_rows):
                    last = act.activation(q_st[b][h][rows, :], rotated[0][rows, :], ACT.Copy)
                last.then_inc(high_done, 1)

            def k_high(s, b, h):
                act.wait_ge(rot_done, 2 * s + 2)
                for dup in pair_rows:
                    last = act.activation(k_hh[b][h][dup, :], rotated[1][pair_rows[h], :], ACT.Copy)
                if h == 1:
                    last.then_inc(high_done, 1)

            def v_copy(s):
                act.wait_ge(projected, 3 * s + 3)
                if later(s, 1):
                    act.wait_ge(v_tr, s)
                act.activation(v_t[:], proj_ps[0][:], ACT.Copy).then_inc(v_copied, 1)

            def v_hi(a, parity):
                act.wait_ge(v_tr, a + 1)
                if later(a, 2):
                    act.wait_ge(pv_done, 2 * a - 2)
                act.activation(v_hl[parity][:, :, 0:4:3, :], proj_ps[1][:].rearrange("p (t h d) -> p t h d", t=QT, h=2),
                               ACT.Copy).then_inc(v_high, 1)

            def exps(n, h, banks=(0, 1, 2)):
                for bank in banks:
                    tiles = SCORE_BANKS[bank]
                    act.wait_ge(maxed, 3 * n + bank + 1)
                    if bank == 0 and later(n, 2):
                        act.wait_ge(pt_tr, 3 * n - 3)
                    for t, col in tiles:
                        width = (t + 1) * P
                        last = act.activation(prob[h][:, P_COL[t]:P_COL[t] + width], score_ps[bank][:, col:col + width],
                                              ACT.Exp, bias=neg_max[h][:, t:t + 1], accum_out=row_sum[h][:, t:t + 1])
                    last.then_inc(expd, 1)

            def pt_hi_parts(n, h, uses=(0, 1, 2)):
                for u in uses:
                    act.wait_ge(pt_tr, 3 * n + u + 1)
                    if u == 0 and later(n, 2):
                        act.wait_ge(pv_done, n - 1)
                    act.activation(pt_hi[h][:, 512 * u:512 * u + PT_WIDTH[u]], pt_ps[u % 2][:, 0:PT_WIDTH[u]],
                                   ACT.Copy).then_inc(pt_high, 1)

            def copy_low_half(n, h):
                act.wait_ge(pv_done, n + 1)
                if later(n, 1):
                    act.wait_ge(merged, n)
                act.activation(low_half[pair_rows[h], :], out_ps[pair_rows[1 - h], :], ACT.Copy).then_inc(half_copied, 1)

            def wo_hi(k):
                act.wait_ge(wo_in[k % 3], 16 * (k // 3 + 1))
                act.wait_ge(projected, 3 * (STEPS - 1 + k // 4))
                act.activation(wo_part[k][PHI], wo_raw[:, k % 3, :], ACT.Copy).then_inc(wo_high, 1)

            def att_hi(n, p):
                if isinstance(n, int):
                    act.wait_ge(projected, 3 * (STEPS - 1) + n + 1)
                else:
                    act.wait_ge(y_mm, n - 1)
                act.wait_ge(att_in[p], 8 * (n - p) + 16)
                act.activation(w_hi[p][:].rearrange("p k n -> p (k n)"), att_raw[:, p, :], ACT.Copy).then_inc(att_high, 1)

            def silu(n, p):
                act.wait_ge(xz_in[p], 16 * (n - p) + 32)
                act.activation(z_tile[:, p, :], z_tile[:, p, :], ACT.Silu).then_inc(silu_done, 1)

            def step(i, s, b, spare):
                if later(s, 1):
                    v_hi(s - 1, 1 - b)
                if later(s, 2):
                    pt_hi_parts(2 * s - 3, 1, (2,))
                    copy_low_half(2 * s - 3, 1)
                if later(s, 1):
                    exps(2 * s - 2, 0)
                q_high(s, b)
                if b == 1:
                    spare(i, 0)
                if later(s, 1):
                    pt_hi_parts(2 * s - 2, 0, (0, 1))
                    if spare is output_weights and b == 1:
                        att_hi(0, 0)
                    exps(2 * s - 1, 1, (0, 1))
                    pt_hi_parts(2 * s - 2, 0, (2,))
                    exps(2 * s - 1, 1, (2,))
                k_high(s, b, 0)
                v_copy(s)
                k_high(s, b, 1)
                if later(s, 1):
                    copy_low_half(2 * s - 2, 0)
                    pt_hi_parts(2 * s - 1, 1, (0, 1))
                if b == 1:
                    spare(i, 1)
                    spare(i, 2)

            def next_weights(i, m):
                weights_high(i + 1, m)

            def output_weights(i, m):
                if m == 0:
                    wo_hi(0)
                    wo_hi(1)
                elif m == 1:
                    wo_hi(2)
                    wo_hi(3)

            step(0, 0, 0, next_weights)
            step(0, 1, 1, next_weights)
            with act.Fori(1, STEPS // 2 - 1) as i:
                step(i, 2 * i, 0, next_weights)
                step(i, 2 * i + 1, 1, next_weights)
            i = STEPS // 2 - 1
            step(i, 2 * i, 0, output_weights)
            step(i, 2 * i + 1, 1, output_weights)
            s = STEPS
            v_hi(s - 1, 1)
            pt_hi_parts(2 * s - 3, 1, (2,))
            copy_low_half(2 * s - 3, 1)
            wo_hi(4)
            exps(2 * s - 2, 0)
            wo_hi(5)
            exps(2 * s - 1, 1)
            pt_hi_parts(2 * s - 2, 0)
            wo_hi(6)
            copy_low_half(2 * s - 2, 0)
            wo_hi(7)
            pt_hi_parts(2 * s - 1, 1)
            att_hi(1, 1)
            copy_low_half(2 * s - 1, 1)
            silu(0, 0)
            silu(1, 1)
            with act.Fori(1, TILES // 2) as i:
                for p in range(2):
                    att_hi(2 * i + p, p)
                    silu(2 * i + p, p)

        @block.vector
        def _(dve):
            def rotate_read(s, c):
                dve.wait_ge(projected, 3 * s + c + 1)
                if later(s, 1):
                    dve.wait_ge(rot_done, 2 * s + c - 1)
                dve.tensor_tensor(turned[c][:], proj_ps[c][:], rope[:, 2 * c, :], ALU.mult)
                dve.stream_shuffle(swapped[c][:], proj_ps[c][:], swap_mask).then_inc(rot_read, 1)

            def q_low(s, b):
                dve.wait_ge(high_done, 2 * s + 1)
                for h, rows in enumerate(pair_rows):
                    last = dve.tensor_tensor(q_st[b][h][pair_rows[1 - h], :], rotated[0][rows, :], raw(q_st[b][h][rows, :]),
                                             ALU.subtract)
                last.then_inc(qk_ready, 1)

            def k_low(s, b):
                dve.wait_ge(high_done, 2 * s + 2)
                for h, rows in enumerate(pair_rows):
                    last = dve.tensor_tensor(k_l0[b][h][rows, :], rotated[1][rows, :], raw(k_hh[b][h][rows, :]), ALU.subtract)
                last.then_inc(qk_ready, 1)

            def v_low(a, parity):
                dve.wait_ge(v_high, a + 1)
                dve.tensor_tensor(v_hl[parity][:, :, 1:3, :], proj_ps[1][:].rearrange("p (t h d) -> p t h d", t=QT, h=2),
                                  raw(v_hl[parity][:, :, 0:4:3, :]), ALU.subtract).then_inc(v_ready, 1)

            def maxima(n, h, banks=(0, 1, 2)):
                for bank in banks:
                    tiles = SCORE_BANKS[bank]
                    dve.wait_ge(scored, 3 * n + bank + 1)
                    for t, col in tiles:
                        diag = score_ps[bank][:, col + t * P:col + (t + 1) * P]
                        last = dve.tensor_tensor(diag, diag, keep["causal"][:], ALU.add)
                    last.then_inc(masked, 1)
                    dve.wait_ge(masked, 3 * n + bank + 1)
                    for t, col in tiles:
                        last = dve.tensor_reduce(neg_max[h][:, t:t + 1], score_ps[bank][:, col:col + (t + 1) * P], AX.X,
                                                 ALU.max, negate=True)
                    last.then_inc(maxed, 1)

            def normalise(n, h):
                dve.wait_ge(expd, 3 * n + 3)
                dve.reciprocal(inv_sum[h][:], row_sum[h][:]).then_inc(inverted, 1)
                dve.wait_ge(inverted, n + 1)
                for t in (1, 0, 2, 3):
                    part = prob[h][:, P_COL[t]:P_COL[t] + (t + 1) * P]
                    last = dve.tensor_scalar(part, part, inv_sum[h][:, t:t + 1], None, ALU.mult)
                last.then_inc(normed, 1)

            def pt_low_parts(n, h, uses=(0, 1, 2)):
                for u in uses:
                    dve.wait_ge(pt_high, 3 * n + u + 1)
                    cols = slice(512 * u, 512 * u + PT_WIDTH[u])
                    dve.tensor_tensor(pt_lo[h][:, cols], pt_ps[u % 2][:, 0:PT_WIDTH[u]], raw(pt_hi[h][:, cols]),
                                      ALU.subtract).then_inc(pt_ready, 1)

            def merge(a, n, h, parity):
                dve.wait_ge(half_copied, n + 1)
                if h == 0 and later(a, 2):
                    dve.wait_ge(att_out[parity], 16 * ((a - parity) // 2))
                rows = pair_rows[h]
                dve.tensor_tensor(att_t[parity][rows, :], out_ps[rows, :], low_half[rows, :], ALU.add).then_inc(merged, 1)

            def step(i, s, b):
                if later(s, 1):
                    v_low(s - 1, 1 - b)
                if later(s, 2):
                    pt_low_parts(2 * s - 3, 1, (2,))
                rotate_read(s, 0)
                if later(s, 2):
                    merge(s - 2, 2 * s - 3, 1, b)
                if later(s, 1):
                    maxima(2 * s - 2, 0)
                    normalise(2 * s - 2, 0)
                q_low(s, b)
                rotate_read(s, 1)
                if later(s, 1):
                    maxima(2 * s - 1, 1, (0,))
                    pt_low_parts(2 * s - 2, 0, (0,))
                    maxima(2 * s - 1, 1, (1, 2))
                    pt_low_parts(2 * s - 2, 0, (1, 2))
                    normalise(2 * s - 1, 1)
                k_low(s, b)
                if later(s, 1):
                    pt_low_parts(2 * s - 1, 1, (0, 1))
                    merge(s - 1, 2 * s - 2, 0, 1 - b)

            dve.wait_ge(keep["z_add"], BATCH * QT)
            for p in range(2):
                dve.memset(raw(k_l0[p][0][HEAD_DIM:P, :]), 0.0).then_inc(zeroed, 1)
                dve.memset(raw(k_l0[p][1][0:HEAD_DIM, :]), 0.0).then_inc(zeroed, 1)
            dve.wait_ge(rope_in, 16)
            loop(dve, step)

            def wo_lo(k):
                dve.wait_ge(wo_high, k + 1)
                dve.tensor_tensor(wo_part[k][PLO], wo_raw[:, k % 3, :], raw(wo_part[k][PHI]), ALU.subtract).then_inc(wo_low_dve, 1)

            def gate(n, p):
                dve.wait_ge(y_mm, n + 1)
                dve.wait_ge(silu_done, n + 1)
                if later(n, 2):
                    dve.wait_ge(y_out[p], 8 * (n - p))
                elif n == 0:
                    dve.wait_ge(pt_tr, 6 * STEPS)
                for o in range(2):
                    cols = slice(o * HALF, (o + 1) * HALF)
                    dve.tensor_tensor(y_tile[p][:, cols], y_ps[p][o][:], z_tile[:, p, cols], ALU.mult).then_inc(y_mul, 1)
                dve.wait_ge(y_mul, 2 * n + 2)
                dve.tensor_tensor(y_tile[p], y_tile[p], x_tile[:, p, :], ALU.add).then_inc(y_add, 1)

            wo_lo(2)
            s = STEPS
            v_low(s - 1, 1)
            pt_low_parts(2 * s - 3, 1, (2,))
            wo_lo(3)
            merge(s - 2, 2 * s - 3, 1, 0)
            maxima(2 * s - 2, 0)
            normalise(2 * s - 2, 0)
            maxima(2 * s - 1, 1)
            normalise(2 * s - 1, 1)
            pt_low_parts(2 * s - 2, 0)
            wo_lo(5)
            merge(s - 1, 2 * s - 2, 0, 1)
            wo_lo(7)
            pt_low_parts(2 * s - 1, 1)
            merge(s - 1, 2 * s - 1, 1, 1)
            gate(0, 0)
            gate(1, 1)
            with dve.Fori(1, TILES // 2) as i:
                for p in range(2):
                    gate(2 * i + p, p)

        @block.gpsimd
        def _(pool):
            def rotate(s, c):
                pool.wait_ge(rot_read, 2 * s + c + 1)
                pool.tensor_tensor(swapped[c][:], swapped[c][:], rope[:, 2 * c + 1, :], ALU.mult).then_inc(rot_a, 1)
                pool.wait_ge(rot_a, 2 * s + c + 1)
                if later(s, 1):
                    pool.wait_ge(qk_ready, 2 * s + c - 1)
                pool.tensor_tensor(rotated[c][:], swapped[c][:], turned[c][:], ALU.add).then_inc(rot_done, 1)

            def weights_low(idx, m):
                pool.wait_ge(w_high, 3 * idx + m + 1)
                pool.tensor_tensor(w_lo[m][:], w_raw[m], raw(w_hi[m][:]), ALU.subtract).then_inc(w_ready[m], 1)

            def wo_lo(k):
                pool.wait_ge(wo_high, k + 1)
                pool.tensor_tensor(wo_part[k][PLO], wo_raw[:, k % 3, :], raw(wo_part[k][PHI]), ALU.subtract).then_inc(wo_low_pool, 1)

            def att_lo(n, p):
                pool.wait_ge(att_high, n + 1)
                pool.tensor_tensor(w_lo[p][:].rearrange("p k n -> p (k n)"), att_raw[:, p, :],
                                   raw(w_hi[p][:]).rearrange("p k n -> p (k n)"), ALU.subtract).then_inc(att_split, 1)

            def step(i, s, b, last=False):
                rotate(s, 0)
                if b == 1 and last:
                    wo_lo(0)
                elif b == 1:
                    weights_low(i + 1, 0)
                rotate(s, 1)
                if b == 1 and last:
                    wo_lo(1)
                    att_lo(0, 0)
                elif b == 1:
                    weights_low(i + 1, 1)
                    weights_low(i + 1, 2)

            pool.wait_ge(rope_in, 16)
            step(0, 0, 0)
            step(0, 1, 1)
            with pool.Fori(1, STEPS // 2 - 1) as i:
                step(i, 2 * i, 0)
                step(i, 2 * i + 1, 1)
            i = STEPS // 2 - 1
            step(i, 2 * i, 0)
            step(i, 2 * i + 1, 1, last=True)
            wo_lo(4)
            wo_lo(6)
            att_lo(1, 1)
            with pool.Fori(1, TILES // 2) as i:
                for p in range(2):
                    att_lo(2 * i + p, p)


def later(count, least):
    return not isinstance(count, int) or count >= least


def build(nc, x, wq, wk, wv, wo, weight, bias, gate_w, in_scale, out_scale, rope, out):
    io = {"x": x.rearrange("b s e -> (b s) e"), "wq": wq, "wk": wk, "wv": wv, "wo": wo, "weight": weight, "bias": bias,
          "gate_w": gate_w, "in_scale": in_scale, "out_scale": out_scale, "rope": rope}
    xn_store = nc.dram_tensor("xn_store", (2, P, 2, KT, SEQ), F32, kind="Internal").ap()
    z_store = nc.dram_tensor("z_store", (BATCH * SEQ, EMBED), F32, kind="Internal").ap()
    att_store = nc.dram_tensor("att_store", (STEPS, P, SEQ), F32, kind="Internal").ap()
    with ExitStack() as whole:
        def sb(ctx, name, shape, dt):
            return ctx.enter_context(nc.sbuf_tensor(name, shape, dt))

        def sem(name):
            return whole.enter_context(nc.semaphore(name))

        block = whole.enter_context(nc.Block())
        keep = {"sem": sem, "ident": sb(whole, "ident", [P, P], F32), "ident_r": sb(whole, "ident_r", [P, P], F32R),
                "ident_bf": sb(whole, "ident_bf", [P, P], BF16), "causal": sb(whole, "causal", [P, P], F32)}
        with ExitStack() as with_xn:
            keep["w_stage"] = sb(with_xn, "w_stage", [P, 3, EMBED], F32)
            keep["z"] = sb(with_xn, "z", [P, 2, EMBED], F32)
            with ExitStack() as early:
                keep["xn_full"] = sb(early, "xn_full", [P, KT, SEQ], F32)
                keep["x_tiles"] = sb(early, "x_tiles", [P, 3, EMBED], F32)
                keep["xs_full"] = sb(early, "xs_full", [P, 2, SEQ], F32)
            keep["w_hi"] = [sb(with_xn, f"w_hi{m}", [P, KT, P], F32R) for m in range(3)]
            keep["w_lo"] = [sb(with_xn, f"w_lo{m}", [P, KT, P], F32R) for m in range(3)]
            keep["rope"] = sb(with_xn, "rope_table", [P, 4, SEQ], F32)
            keep["z_out"] = [sem(f"z_out{i}") for i in range(2)]
            keep["w_in"] = [sem(f"w_in{m}") for m in range(3)]
            keep["w_high"], keep["w_ready"] = sem("w_high"), [sem(f"w_ready{m}") for m in range(3)]
            keep["rope_in"], keep["z_add"], keep["xn_ok"] = sem("rope_in"), sem("z_add"), sem("xn_ok")
            xn = [[sb(with_xn, f"xn{b}_{part}", [P, KT, SEQ], F32R) for part in ("hi", "lo")] for b in range(2)]
            with ExitStack() as with_ffn:
                keep["sign_t"] = sb(with_ffn, "sign_t", [P, KT, EMBED], F32R)
                keep["chan_in"] = sb(with_ffn, "chan_in", [P, EMBED], F32R)
                keep["chan_out"] = sb(with_ffn, "chan_out", [P, EMBED], F32R)
                keep["gate_t"] = sb(with_ffn, "gate_t", [P, KT, 2 * EXPERTS], F32R)
                keep["bias"] = sb(with_ffn, "bias", [P, EMBED], F32)
                ffn_block(nc, block, io, keep, xn, xn_store, z_store)
            attention_block(nc, block, io, keep, xn, xn_store, z_store, att_store, out.rearrange("b s e -> (b s) e"))


_INS = ['L0_attn_hidden_states', 'L0_attn_Wq', 'L0_attn_Wk', 'L0_attn_Wv', 'L0_attn_Wo', 'L0_ffn_weight', 'L0_ffn_bias',
        'L0_ffn_gate_w', 'L0_ffn_in_channel_scale', 'L0_ffn_out_channel_scale']


def rope_table():
    import numpy as np
    inv_freq = (np.float32(1.0) / np.float32(10000.0) ** (np.arange(0, HEAD_DIM, 2, dtype=np.float32) / np.float32(HEAD_DIM))).astype(np.float32)
    angle = (np.arange(SEQ, dtype=np.float32)[None, :] * inv_freq[:, None]).astype(np.float32)
    angle = np.tile(np.repeat(angle, 2, axis=0), (2, 1))
    cos, sin = np.cos(angle).astype(np.float32), np.sin(angle).astype(np.float32)
    return np.stack([cos * np.float32(0.125), sin * np.float32(0.125), cos, sin]).astype(np.float32)


def kernel(**inputs):
    import numpy as _np
    import concourse.bacc as _bacc
    from concourse import mybir as _mybir
    from concourse.bass_utils import run_bass_kernel_spmd as _run

    nc = _bacc.Bacc("TRN2", target_bir_lowering=False, num_devices=1)
    arrays, args = {}, []
    for name in _INS:
        a = _np.ascontiguousarray(inputs[name])
        arrays[f"in_{name}_dram"] = a
        args.append(nc.dram_tensor(f"in_{name}_dram", a.shape, _mybir.dt.from_np(a.dtype), kind="ExternalInput").ap())
    rope = rope_table()
    arrays["in_rope_dram"] = rope
    args.append(nc.dram_tensor("in_rope_dram", rope.shape, _mybir.dt.float32, kind="ExternalInput").ap())
    args.append(nc.dram_tensor("out_0_dram", (BATCH, SEQ, EMBED), _mybir.dt.float32, kind="ExternalOutput").ap())
    build(nc, *args)
    r = _run(nc, [arrays], core_ids=[0])
    return r.results[0]["out_0_dram"]
```
